# Optimizing a Trainium2 kernel written in Bass

```python
import numpy as np
import jax
import jax.numpy as jnp

def _softmax(x, axis=-1):
    return jax.nn.softmax(x, axis=axis)

def _gelu(x):
    return jax.nn.gelu(x, approximate=True)

def _silu(x):
    return jax.nn.silu(x)

def _sigmoid(x):
    return jax.nn.sigmoid(x)

def _layernorm(x, axis=-1, eps=1e-05):
    m = jnp.mean(x, axis=axis, keepdims=True)
    v = jnp.var(x, axis=axis, keepdims=True)
    return (x - m) / jnp.sqrt(v + eps)

def _scatter_add(tgt, idx, src, axis=0):
    return tgt.at[idx].add(src)

def _segment_sum(src, seg, n):
    return jax.ops.segment_sum(src, seg, n)
kernel_name = 'mk_prb_d1_jaxref_r8_4bef2e'

def setup_inputs(seed: int=0):
    np.random.seed(seed)
    _w = jnp.asarray

    def _L0_attn_setup():
        import jax, jax.numpy as jnp
        import numpy as np
        N_HEAD = 16
        HEAD_SIZE = 128
        EMBED = 128
        MULTI_HEAD_SIZE = HEAD_SIZE // N_HEAD
        B, S = (4, 256)
        key = jax.random.key(seed)
        k1, k2, k3, k4 = jax.random.split(key, 4)
        x = jax.random.normal(k1, (B, S, EMBED), dtype=jnp.float32)
        w_qkv = jax.random.normal(k2, (3 * HEAD_SIZE, EMBED), dtype=jnp.float32) * 0.02
        w_proj = jax.random.normal(k3, (EMBED, HEAD_SIZE), dtype=jnp.float32) * 0.02
        b_proj = jax.random.normal(k4, (EMBED,), dtype=jnp.float32) * 0.02
        return {'x': x, 'w_qkv': w_qkv, 'w_proj': w_proj, 'b_proj': b_proj}
    _L0_attn_in = _L0_attn_setup()

    def _L0_ffn_setup():
        import jax, jax.numpy as jnp
        import numpy as np
        D_IN, D_H, D_OUT = (128, 128, 128)
        D_MOE = 512
        N_EXPERTS = 8
        TOP_K = 2
        key = jax.random.key(seed)
        ks = jax.random.split(key, 10)
        s = lambda d: 1.0 / np.sqrt(d)
        x = jax.random.normal(ks[0], (2, 256, D_IN), dtype=jnp.float32)
        W_in = jax.random.normal(ks[1], (D_IN, D_H), dtype=jnp.float32) * s(D_IN)
        b_in = jnp.zeros((D_H,), jnp.float32)
        W_gate = jax.random.normal(ks[2], (D_H, N_EXPERTS), dtype=jnp.float32) * s(D_H)
        b_gate = jnp.zeros((N_EXPERTS,), jnp.float32)
        W1 = jax.random.normal(ks[3], (N_EXPERTS, D_H, D_MOE), dtype=jnp.float32) * s(D_H)
        b1 = jnp.zeros((N_EXPERTS, D_MOE), jnp.float32)
        W2 = jax.random.normal(ks[4], (N_EXPERTS, D_MOE, D_H), dtype=jnp.float32) * s(D_MOE)
        b2 = jnp.zeros((N_EXPERTS, D_H), jnp.float32)
        W_out = jax.random.normal(ks[5], (D_H, D_OUT), dtype=jnp.float32) * s(D_H)
        b_out = jnp.zeros((D_OUT,), jnp.float32)
        return {'x': x, 'W_in': W_in, 'b_in': b_in, 'W_gate': W_gate, 'b_gate': b_gate, 'W1': W1, 'b1': b1, 'W2': W2, 'b2': b2, 'W_out': W_out, 'b_out': b_out}
    _L0_ffn_in = _L0_ffn_setup()
    _d = {'L0_attn_x': _L0_attn_in['x'], 'L0_attn_w_qkv': _L0_attn_in['w_qkv'], 'L0_attn_w_proj': _L0_attn_in['w_proj'], 'L0_attn_b_proj': _L0_attn_in['b_proj'], 'L0_ffn_W_in': _L0_ffn_in['W_in'], 'L0_ffn_b_in': _L0_ffn_in['b_in'], 'L0_ffn_W_gate': _L0_ffn_in['W_gate'], 'L0_ffn_b_gate': _L0_ffn_in['b_gate'], 'L0_ffn_W1': _L0_ffn_in['W1'], 'L0_ffn_b1': _L0_ffn_in['b1'], 'L0_ffn_W2': _L0_ffn_in['W2'], 'L0_ffn_b2': _L0_ffn_in['b2'], 'L0_ffn_W_out': _L0_ffn_in['W_out'], 'L0_ffn_b_out': _L0_ffn_in['b_out']}
    _x0 = _d['L0_attn_x']
    _d['L0_attn_x'] = jax.random.normal(jax.random.fold_in(jax.random.key(seed), 1), (1, 2048, 128), dtype=_x0.dtype)
    del _x0
    return _d

def reference(L0_attn_x, L0_attn_w_qkv, L0_attn_w_proj, L0_attn_b_proj, L0_ffn_W_in, L0_ffn_b_in, L0_ffn_W_gate, L0_ffn_b_gate, L0_ffn_W1, L0_ffn_b1, L0_ffn_W2, L0_ffn_b2, L0_ffn_W_out, L0_ffn_b_out):

    def _L0_attn_ref(x, w_qkv, w_proj, b_proj):
        import jax, jax.numpy as jnp
        import numpy as np
        N_HEAD = 16
        HEAD_SIZE = 128
        EMBED = 128
        MULTI_HEAD_SIZE = HEAD_SIZE // N_HEAD
        B, S = (4, 256)
        qkv = jnp.einsum('bse,he->bsh', x, w_qkv)
        q, k, v = jnp.split(qkv, 3, axis=-1)
        scale = 1.0 / np.sqrt(MULTI_HEAD_SIZE).astype(np.float32)
        scores = jnp.einsum('bqh,bkh->bqk', q, k) * scale
        probs = jax.nn.softmax(scores, axis=-1)
        out = jnp.einsum('bqk,bkh->bqh', probs, v)
        Bn, Sn, H = out.shape
        out = jnp.swapaxes(out, 1, 2).reshape(Bn, Sn, H)
        out = jnp.einsum('bsh,eh->bse', out, w_proj) + b_proj
        return out

    def _L0_ffn_ref(x, W_in, b_in, W_gate, b_gate, W1, b1, W2, b2, W_out, b_out):
        import jax, jax.numpy as jnp
        import numpy as np
        D_IN, D_H, D_OUT = (128, 128, 128)
        D_MOE = 512
        N_EXPERTS = 8
        TOP_K = 2
        B, S, _ = x.shape
        h = x @ W_in + b_in
        t = h.reshape(B * S, -1)
        logits = t @ W_gate + b_gate
        probs = jax.nn.softmax(logits, axis=-1)
        topv, topi = jax.lax.top_k(probs, TOP_K)
        topv = topv / jnp.sum(topv, axis=-1, keepdims=True)
        route = jnp.zeros_like(probs).at[jnp.arange(t.shape[0])[:, None], topi].set(topv)
        mid = jax.nn.relu(jnp.einsum('nd,edh->neh', t, W1) + b1)
        eout = jnp.einsum('neh,ehd->ned', mid, W2) + b2
        moe_out = jnp.einsum('ne,ned->nd', route, eout)
        out = moe_out.reshape(B, S, -1) @ W_out + b_out
        return out
    x = L0_attn_x
    xn = _layernorm(x, axis=-1)
    x = x + _L0_attn_ref(xn, L0_attn_w_qkv, L0_attn_w_proj, L0_attn_b_proj) + _L0_ffn_ref(xn, L0_ffn_W_in, L0_ffn_b_in, L0_ffn_W_gate, L0_ffn_b_gate, L0_ffn_W1, L0_ffn_b1, L0_ffn_W2, L0_ffn_b2, L0_ffn_W_out, L0_ffn_b_out)
    return x

_drawn_inputs = setup_inputs


def setup_inputs(seed=0):
    import zlib

    import numpy as np

    out = dict(_drawn_inputs(seed))
    spreads = {'L0_ffn_b_in': (0.0, 0.1),
     'L0_ffn_b_gate': (0.0, 0.1),
     'L0_ffn_b1': (0.0, 0.492),
     'L0_ffn_b2': (0.0, 0.356),
     'L0_ffn_b_out': (0.0, 0.1)}
    factors = {'L0_attn_w_qkv': 8.0, 'L0_attn_w_proj': 8.0, 'L0_attn_b_proj': 8.994}
    for name, (base, spread) in spreads.items():
        noise = np.random.default_rng([zlib.crc32(name.encode()), seed]).standard_normal(out[name].shape)
        drawn = base * np.exp(spread * noise) if base else spread * noise
        out[name] = jnp.asarray(drawn.astype(out[name].dtype))
    for name, factor in factors.items():
        out[name] = (out[name] * factor).astype(out[name].dtype)
    return out
```

```python
import concourse.bass as bass
from concourse import mybir
from contextlib import ExitStack

FP32 = mybir.dt.float32
FP32R = mybir.dt.float32r
I32 = mybir.dt.int32
U32 = mybir.dt.uint32
ALU = mybir.AluOpType
ACT = mybir.ActivationFunctionType
AX = mybir.AxisListType


def attention_moe_kernel(nc, x, w_qkv, w_proj, b_proj, w_in, b_in, w_gate, b_gate,
                         w1, b1, w2, b2, w_out, b_out, out):
    P = 128
    S, D = x.shape[1], x.shape[2]
    NT = S // P
    NE, _, DM = w1.shape
    HC = DM // P
    BK = 512
    NR = S // BK
    TB = BK // P
    TOPK = 2
    MT = -(-(TOPK * NT + NE - 1) // TB) * TB
    MB = MT // TB
    HEADS = 16
    SCALE = 1.0 / float(D // HEADS) ** 0.5
    EPS = 1e-5
    LOWEST = -3.0e38

    ctx = ExitStack()
    with ctx:
        def sb(name, shape, dt=FP32):
            return ctx.enter_context(nc.sbuf_tensor(name, shape, dt))

        def sem(name):
            return ctx.enter_context(nc.semaphore(name))

        slots_in = nc.dram_tensor("slots_in", (MT * P, D), FP32, kind="Internal").ap()
        slots_out = nc.dram_tensor("slots_out", (MT * P, D), FP32, kind="Internal").ap()

        x_sb = sb("x_sb", [P, NT, D])
        xnT_hi = sb("xnT_hi", [P, S], FP32R)
        xnT_lo = sb("xnT_lo", [P, S], FP32R)
        v_hi = sb("v_hi", [P, NT, D], FP32R)
        v_lo = sb("v_lo", [P, NT, D], FP32R)
        q_hi = sb("q_hi", [P, BK], FP32R)
        q_lo = sb("q_lo", [P, BK], FP32R)
        probs = sb("probs", [P, S])
        pt_hi = sb("pt_hi", [P, 2, NT, 2 * P], FP32R)
        pt_lo = sb("pt_lo", [P, 2, NT, 2 * P], FP32R)
        oT_all = sb("oT_all", [P, NT, P])
        w1_hi = sb("w1_hi", [P, NE, DM], FP32R)
        w1_lo = sb("w1_lo", [P, NE, DM], FP32R)
        w2_sb = sb("w2_sb", [P, NE * HC * D])
        w1_raw = sb("w1_raw", [P, 2, DM])
        MM, WV, WP, WI, WO = range(5)
        w_hi = sb("w_hi", [P, 5, D], FP32R)
        w_lo = sb("w_lo", [P, 5, D], FP32R)
        ident = sb("ident", [P, P])
        tri = sb("tri", [P, P])
        ones = sb("ones", [P, P])
        bsum = sb("bsum", [P, 3, D])
        bin_col = sb("bin_col", [P, 1])
        wg_sb = sb("wg_sb", [P, NE])
        bg_sb = sb("bg_sb", [P, NE])
        b1_col = sb("b1_col", [P, NE, HC])
        b2_sb = sb("b2_sb", [P, NE, D])
        stats = sb("stats", [P, NT, 6])
        mv = sb("mv", [P, NT, 2])
        veps = sb("veps", [P, NT])
        std = sb("std", [P, NT])
        rstd = sb("rstd", [P, NT])
        newton = sb("newton", [P, NT])
        bank_max = sb("bank_max", [P, 2, NR])
        neg_max = sb("neg_max", [P, 2])
        sums = sb("sums", [P, NT * NR])
        rinv = sb("rinv", [P, NT])
        lg = sb("lg", [P, NT, NE])
        eq = sb("eq", [P, NT, NE])
        one1 = sb("one1", [P, NT, NE])
        one2 = sb("one2", [P, NT, NE])
        both = sb("both", [P, NT, NE])
        desc = sb("desc", [P, NE])
        first_tile = sb("first_tile", [P, NE, NT])
        tot = sb("tot", [P, NE, NT])
        cum = sb("cum", [P, NE, NT])
        thr = sb("thr", [P, NT])
        tiles_e = sb("tiles_e", [P, NE])
        tiles_c = sb("tiles_c", [P, NE])
        tiles_x = sb("tiles_x", [P, NE])
        tile_no = sb("tile_no", [P, MT])
        cmp = sb("cmp", [P, MT, NE])
        texp_f = sb("texp_f", [P, MT])
        texp = sb("texp", [P, MT], I32)
        top1 = sb("top1", [P, NT])
        top2 = sb("top2", [P, NT])
        pick = sb("pick", [P, NT])
        gap = sb("gap", [P, NT])
        e2 = sb("e2", [P, NT])
        den = sb("den", [P, NT])
        gate1 = sb("gate1", [P, NT])
        gate2 = sb("gate2", [P, NT])
        slot1 = sb("slot1", [P, NT], I32)
        slot2 = sb("slot2", [P, NT], I32)
        xgT_hi = sb("xgT_hi", [P, BK], FP32R)
        xgT_lo = sb("xgT_lo", [P, BK], FP32R)
        mid = sb("mid", [P, 2, DM])
        xn = probs[:, 0:2 * BK].rearrange("p (b j e) -> p b j e", b=2, e=D)
        xg = w1_raw[:, 0, :].rearrange("p (j d) -> p j d", d=D)
        y_sb = w1_raw[:, 1, :].rearrange("p (j d) -> p j d", d=D)
        tT = w2_sb[:, 0:S]
        w_raw = w2_sb[:, S:S + 6 * D].rearrange("p (t e) -> p t e", e=D)
        t_rows = oT_all[:, :, :]
        w2v = w2_sb[:, :].rearrange("p (e c d) -> p e c d", e=NE, d=D)
        ZB = 8
        moe = w2_sb[:, 0:S].rearrange("p (j d) -> p j d", d=D)
        z = w2_sb[:, S:2 * S].rearrange("p (b t d) -> p b t d", b=ZB, d=D)
        o_sb = mid[:, :, :].rearrange("p b (j d) -> p b j d", d=D)
        o_hi = w1_hi[:, 0:2, :].rearrange("p b (j d) -> p b j d", d=D)
        o_lo = w1_lo[:, 0:2, :].rearrange("p b (j d) -> p b j d", d=D)
        moeT_hi = w1_hi[:, NE - NR:NE, :].rearrange("p a b -> p (a b)")
        moeT_lo = w1_lo[:, NE - NR:NE, :].rearrange("p a b -> p (a b)")

        midT = oT_all[:, NT // 2:NT, :].rearrange("p (b c) n -> p b c n", b=2)

        b1_rows = mid[0:NE * HC, 0, 0:P]

        def raw(ap):
            return ap.bitcast(FP32)

        ps_s = ctx.enter_context(nc.psum_tensor("ps_s", [P, NR, BK], FP32))
        ps_t = ctx.enter_context(nc.psum_tensor("ps_t", [P, 2, BK], FP32))
        ps_o = ctx.enter_context(nc.psum_tensor("ps_o", [P, BK], FP32))
        ps_m = ctx.enter_context(nc.psum_tensor("ps_m", [P, BK], FP32))

        Z = {n: sem(n) for n in """
            w_loaded b_loaded consts zero_ready zeroed ln_link ln_std_in std_ready ln_ready xn_ready
            xT_done xT_hi xT_lo wT_done w_hi_ready w_lo_ready x_biased
            v_done v_hi_ready v_lo_ready rows_done rows_ready tT_done tT_ready logits_done
            q_done q_hi_ready q_lo_ready scores_done part_max neg_max_ready exp_done
            pT_done pt_hi_ready pt_lo_ready pv_done oT_copied
            route_link gap_ready e2_ready both_ready prefix_done slots_ready scattered
            w1_split w2_loaded w1_hi_ready
            xg_loaded xgT_done xgT_hi_ready xgT_lo_ready l1_done l1_copied midT_done midT_ready
            y_done y_ready combined moe_link moeT_done moeT_hi_ready moeT_lo_ready
            sums_link rinv_ready oTT_done o_ready o_hi_ready o_lo_ready out_done out_added stored
            """.split()}
        s_x = [sem(f"x_loaded{r}") for r in range(NR)]
        s_w1 = [sem(f"w1_loaded{r}") for r in range(2)]
        s_y = [sem(f"y_stored{r}") for r in range(2)]
        s_z = [sem(f"z_loaded{r}") for r in range(ZB)]

        def exact(it):
            return isinstance(it, int)

        def tT_bank(r):
            return (ps_o if r % 2 else ps_m)[:, :]

        def moeT_view(t, r):
            return t.rearrange("d (j p) -> d p j", p=P)[:, 32 * r:32 * (r + 1), :]

        def moeT_bank(r):
            return ps_s[:, r, :].rearrange("d (p j) -> d p j", j=NT)

        block = ctx.enter_context(nc.Block())

        @block.sync
        def _(sp):
            xv = x.rearrange("o (p j) e -> p (o j) e", p=P)
            for r in range(NR):
                sp.dma_start(x_sb[:, TB * r:TB * (r + 1), :], xv[:, TB * r:TB * (r + 1), :]).then_inc(s_x[r], 16)
            sp.wait_ge(Z["zero_ready"], 1)
            zero = pt_hi[:, 0, :, :].rearrange("p a b -> p (a b)").bitcast(FP32)
            zv = slots_in.rearrange("(b p r) d -> b p (r d)", p=P, b=2)
            for b in range(2):
                sp.dma_start(zv[b], zero[:, 0:MT // 2 * D]).then_inc(Z["zeroed"], 16)
            for e in range(NE):
                if e >= 2:
                    sp.wait_ge(Z["w1_split"], e - 1)
                sp.dma_start(w1_raw[:, e % 2, :], w1[e]).then_inc(s_w1[e % 2], 16)
            sp.wait_ge(Z["logits_done"], 1)
            sp.wait_ge(Z["w_lo_ready"], 2)
            sp.dma_start(w2v, w2.rearrange("e (c p) d -> p e c d", p=P)).then_inc(Z["w2_loaded"], 16)

            xg_src = slots_in.rearrange("(t p) d -> p t d", p=P)
            y_dst = slots_out.rearrange("(t p) d -> p t d", p=P)

            def load_xg(b):
                sp.dma_start(xg[:, :, :], xg_src[:, bass.ds(b * TB, TB), :]).then_inc(Z["xg_loaded"], 16)

            def store_y(b, h):
                sp.wait_ge(Z["y_ready"], b * TB + (2 * h + 2))
                sp.dma_start(y_dst[:, bass.ds(b * TB + 2 * h, 2), :], y_sb[:, 2 * h:2 * h + 2, :]).then_inc(s_y[h], 16)

            sp.wait_ge(Z["scattered"], 16 * TOPK * NT)
            sp.wait_ge(Z["w1_split"], NE)
            load_xg(0)
            sp.wait_ge(Z["xgT_done"], 1)
            load_xg(1)
            with sp.Fori(0, MB - 2) as b:
                store_y(b, 0)
                sp.wait_ge(Z["xgT_done"], b + 2)
                load_xg(b + 2)
                store_y(b, 1)
            for b in range(MB - 2, MB):
                store_y(b, 0)
                store_y(b, 1)
            ov = out.rearrange("o (p j) e -> p (o j) e", p=P)
            for r in range(NR):
                sp.wait_ge(Z["out_added"], r + 1)
                sp.dma_start(ov[:, TB * r:TB * (r + 1), :], x_sb[:, TB * r:TB * (r + 1), :]).then_inc(Z["stored"], 16)
            sp.wait_ge(Z["stored"], 16 * NR)

        @block.gpsimd
        def _(pool):
            pool.memset(raw(pt_hi[:, 0, :, :]), 0.0).then_inc(Z["zero_ready"], 1)
            pool.memset(ident[:, :], 0.0).then_inc(Z["consts"], 1)
            pool.memset(ones[:, :], 1.0).then_inc(Z["consts"], 1)
            pool.memset(first_tile[:, :, :], 1.0).then_inc(Z["consts"], 1)
            pool.iota(desc[:, :], pattern=[[-1, NE]], base=NE, channel_multiplier=0,
                      allow_small_or_imprecise_dtypes=True).then_inc(Z["consts"], 1)
            pool.iota(thr[:, :], pattern=[[P, NT]], base=0, channel_multiplier=0,
                      allow_small_or_imprecise_dtypes=True).then_inc(Z["consts"], 1)
            pool.iota(tile_no[:, :], pattern=[[1, MT]], base=0, channel_multiplier=0,
                      allow_small_or_imprecise_dtypes=True).then_inc(Z["consts"], 1)
            pool.wait_ge(Z["consts"], 6)
            pool.affine_select(out=ident[:, :], in_=ident[:, :], compare_op=ALU.not_equal, fill=1.0,
                               base=0, pattern=[[-1, P]], channel_multiplier=1).then_inc(Z["consts"], 1)
            pool.affine_select(out=tri[:, :], in_=ones[:, :], compare_op=ALU.is_gt, fill=0.0,
                               base=0, pattern=[[1, P]], channel_multiplier=-1).then_inc(Z["consts"], 1)
            pool.affine_select(out=first_tile[:, :, :], in_=first_tile[:, :, :], compare_op=ALU.is_gt, fill=0.0,
                               base=0, pattern=[[0, NE], [1, NT]], channel_multiplier=0).then_inc(Z["consts"], 1)
            for e in range(NE):
                pool.wait_ge(s_w1[e % 2], 16 * (e // 2 + 1))
                pool.tensor_copy(w1_hi[:, e, :], w1_raw[:, e % 2, :]).then_inc(Z["w1_hi_ready"], 1)
                pool.wait_ge(Z["w1_hi_ready"], e + 1)
                pool.tensor_tensor(w1_lo[:, e, :], w1_raw[:, e % 2, :], raw(w1_hi[:, e, :]),
                                   ALU.subtract).then_inc(Z["w1_split"], 1)
            pool.wait_ge(Z["zeroed"], 32)
            pool.wait_ge(Z["slots_ready"], 2)
            pool.wait_ge(Z["rows_ready"], NR)
            for j in range(NT):
                for s in (slot1, slot2):
                    pool.indirect_dma_start(out=slots_in, out_offset=bass.IndirectOffsetOnAxis(ap=s[:, j:j + 1], axis=0),
                                            in_=t_rows[:, j, :], in_offset=None).then_inc(Z["scattered"], 16)
            pool.wait_ge(Z["b_loaded"], 16 * 7)
            pool.wait_ge(Z["xn_ready"], NT)
            pool.tensor_tensor(bsum[:, 0, :], bsum[:, 0, :], bsum[:, 1, :], ALU.add).then_inc(Z["x_biased"], 1)
            pool.wait_ge(Z["x_biased"], 1)
            pool.tensor_tensor(x_sb[:, :, :], x_sb[:, :, :], bsum[:, 0:1, :].to_broadcast([P, NT, D]),
                               ALU.add).then_inc(Z["x_biased"], 1)
            for h in range(2):
                pool.wait_ge(s_y[h], 16 * MB)
            pool.wait_ge(Z["y_done"], MT)
            for j in range(NT):
                if j >= ZB:
                    pool.wait_ge(Z["combined"], j - ZB + 1)
                for t, s in enumerate((slot1, slot2)):
                    pool.indirect_dma_start(out=z[:, j % ZB, t, :], out_offset=None, in_=slots_out,
                                            in_offset=bass.IndirectOffsetOnAxis(ap=s[:, j:j + 1], axis=0)
                                            ).then_inc(s_z[j % ZB], 16)

        @block.scalar
        def _(act):
            wv_ = w_qkv.rearrange("(t p) e -> p t e", p=P)
            act.dma_start(w_raw[:, 0:3, :], wv_).then_inc(Z["w_loaded"], 16)
            act.dma_start(w_raw[:, 3, :], w_proj).then_inc(Z["w_loaded"], 16)
            act.dma_start(w_raw[:, 4, :], w_in).then_inc(Z["w_loaded"], 16)
            act.dma_start(w_raw[:, 5, :], w_out).then_inc(Z["w_loaded"], 16)
            act.dma_start(b1_rows, b1.rearrange("e (c p) -> (e c) p", p=P)).then_inc(Z["w_loaded"], 16)

            def rows(v, n):
                return v.rearrange("(a n) -> a n", a=1).to_broadcast([P, n])
            act.dma_start(bsum[:, 0, :], rows(b_proj, D)).then_inc(Z["b_loaded"], 16)
            act.dma_start(bsum[:, 1, :], rows(b_out, D)).then_inc(Z["b_loaded"], 16)
            act.dma_start(bsum[:, 2, :], rows(b_in, D)).then_inc(Z["b_loaded"], 16)
            act.dma_start(bg_sb[:, :], rows(b_gate, NE)).then_inc(Z["b_loaded"], 16)
            act.dma_start(bin_col[:, :], b_in.rearrange("(p a) -> p a", a=1)).then_inc(Z["b_loaded"], 16)
            act.dma_start(wg_sb[:, :], w_gate).then_inc(Z["b_loaded"], 16)
            act.dma_start(b2_sb[:, :, :].rearrange("p e d -> p (e d)"),
                          b2.rearrange("(a e) d -> a (e d)", a=1).to_broadcast([P, NE * D])).then_inc(Z["b_loaded"], 16)

            act.wait_ge(Z["wT_done"], 1)
            act.activation(w_hi[:, 0:3, :], ps_m[:, 0:3 * D].rearrange("p (t n) -> p t n", t=3),
                           ACT.Copy).then_inc(Z["w_hi_ready"], 1)
            act.activation(b1_col[:, :, :].rearrange("p e c -> p (e c)"), ps_m[:, 3 * D:3 * D + NE * HC],
                           ACT.Copy).then_inc(Z["w_hi_ready"], 1)
            act.activation(w_hi[:, 3:5, :], w_raw[:, 4:6, :], ACT.Copy).then_inc(Z["w_hi_ready"], 1)
            act.wait_ge(Z["ln_std_in"], 1)
            act.activation(std[:, :], veps[:, :], ACT.Sqrt).then_inc(Z["std_ready"], 1)
            xh = xnT_hi[:, :].rearrange("e (p j) -> e j p", j=NT)

            def split_v_t(r):
                act.wait_ge(Z["v_done"], r + 1)
                act.activation(v_hi[:, TB * r:TB * (r + 1), :], ps_s[:, r % 2, :].rearrange("p (j d) -> p j d", d=D),
                               ACT.Copy).then_inc(Z["v_hi_ready"], 1)
                act.wait_ge(Z["b_loaded"], 16 * 7)
                act.wait_ge(Z["tT_done"], r + 1)
                act.activation(tT[:, BK * r:BK * (r + 1)], tT_bank(r), ACT.Identity,
                               bias=bin_col[:, 0:1]).then_inc(Z["tT_ready"], 1)

            for r in range(NR):
                act.wait_ge(Z["xT_done"], r + 1)
                act.activation(xh[:, TB * r:TB * (r + 1), :], ps_t[:, r % 2, :].rearrange("e (j p) -> e j p", p=P),
                               ACT.Copy).then_inc(Z["xT_hi"], 1)
            for r in range(NR):
                split_v_t(r)

            def q_split(n):
                act.wait_ge(Z["q_done"], n)
                act.activation(q_hi[:, :], ps_m[:, :], ACT.Copy, scale=SCALE).then_inc(Z["q_hi_ready"], 1)

            def step(it, c, scores=True, tr=True):
                i = it * TB + c
                for b in range(NR):
                    if scores:
                        if b == 0:
                            act.wait_ge(Z["neg_max_ready"], i + 1)
                        if not (exact(it) and i < 1):
                            act.wait_ge(Z["pT_done"], (i - 1) * NR + (b + 1))
                        act.activation(probs[:, BK * b:BK * (b + 1)], ps_s[:, b, :], ACT.Exp,
                                       bias=neg_max[:, c % 2:c % 2 + 1],
                                       accum_out=sums[:, bass.ds(i * NR + b, 1)]).then_inc(Z["exp_done"], 1)
                    if tr:
                        if b == 0 and (c - 1) % 2 == 0 and not (exact(it) and i < 5):
                            act.wait_ge(Z["pv_done"], it * 2 + ((c - 1) // 2 - 1))
                        act.wait_ge(Z["pT_done"], (i - 1) * NR + (b + 1))
                        act.activation(pt_hi[:, (c - 1) // 2 % 2, TB * b:TB * (b + 1), P * ((c - 1) % 2):P * ((c - 1) % 2 + 1)],
                                       ps_t[:, b % 2, :].rearrange("k (c q) -> k c q", q=P),
                                       ACT.Copy).then_inc(Z["pt_hi_ready"], 1)

            def copy_o(g):
                act.wait_ge(Z["pv_done"], g + 1)
                act.activation(oT_all[:, bass.ds(g * 2, 2), :], ps_o[:, 0:2 * P].rearrange("p (a b) -> p a b", a=2),
                               ACT.Copy).then_inc(Z["oT_copied"], 1)

            q_split(1)
            act.wait_ge(Z["zeroed"], 32)
            step(0, 0, tr=False)
            act.wait_ge(Z["gap_ready"], 1)
            act.activation(e2[:, :], gap[:, :], ACT.Exp).then_inc(Z["e2_ready"], 1)
            step(0, 1)
            step(0, 2)
            q_split(2)
            step(0, 3)
            step(0, 4)
            act.wait_ge(Z["scattered"], 16 * TOPK * NT)
            copy_o(0)
            step(0, 5)
            step(0, 6)
            copy_o(1)

            def xgT_split(b):
                act.wait_ge(Z["xgT_done"], b + 1)
                if not (exact(b) and b < 1):
                    act.wait_ge(Z["l1_done"], b * TB)
                act.activation(xgT_hi[:, :], ps_m[:, :], ACT.Copy).then_inc(Z["xgT_hi_ready"], 1)

            def moe_relu(b, u):
                i = b * TB + u
                e = act.value_load(texp[0:1, bass.ds(i - 1, 1)], min_val=0, max_val=NE - 1)
                act.wait_ge(Z["midT_done"], i)
                if not (exact(b) and i < 3):
                    act.wait_ge(Z["y_done"], i - 2)
                for c in range(HC):
                    act.activation(midT[:, (u - 1) % 2, c, :], ps_t[:, (u - 1) % 2, P * c:P * (c + 1)], ACT.Relu,
                                   bias=b1_col[:, bass.ds(e, 1), c]).then_inc(Z["midT_ready"], 1)

            xgT_split(0)
            act.wait_ge(Z["slots_ready"], 2)

            def moe_batch(b, last=False, start=0):
                for u in range(start, TB):
                    if u == TB - 1 and not last:
                        xgT_split(b + 1)
                    moe_relu(b, u)
            moe_batch(0, start=1)
            with act.Fori(1, MB - 1) as b:
                moe_batch(b)
            moe_batch(MB - 1, last=True)
            moe_relu(MB, 0)

            def attention_group(it):
                q_split(it + 2)
                step(it, 3)
                step(it, 4)
                copy_o(it * 2)
                step(it, 5)
                step(it, 6)
                copy_o(it * 2 + 1)

            with act.Fori(1, NR - 1) as it:
                attention_group(it)
            step(NR - 1, 3)
            step(NR - 1, 4, scores=False)
            copy_o(NT // 2 - 2)
            for r in range(NR):
                act.wait_ge(Z["moeT_done"], r + 1)
                act.activation(moeT_view(moeT_hi, r), moeT_bank(r), ACT.Copy).then_inc(Z["moeT_hi_ready"], 1)
            copy_o(NT // 2 - 1)
            for r in range(NR):
                act.wait_ge(Z["o_ready"], r + 1)
                if r >= 2:
                    act.wait_ge(Z["out_done"], r - 1)
                act.activation(o_hi[:, r % 2, :, :], o_sb[:, r % 2, :, :], ACT.Copy).then_inc(Z["o_hi_ready"], 1)

        @block.vector
        def _(dve):
            count = {"ln": 0, "route": 0, "moe": 0, "sums": 0}

            def link(key, inst):
                count[key] += 1
                s = Z[key + "_link"]
                inst.then_inc(s, 1)
                dve.wait_ge(s, count[key])

            for r in range(NR):
                dve.wait_ge(s_x[r], 16)
                for j in range(TB * r, TB * (r + 1)):
                    last = dve.bn_stats(stats[:, j, :], x_sb[:, j, :])
                    last.then_inc(Z["ln_link"], 1)
            count["ln"] = NT
            for j in range(NT):
                if j % TB == 0:
                    dve.wait_ge(Z["ln_link"], j + TB)
                last = dve.bn_aggr(mv[:, j, :], stats[:, j, :])
            link("ln", last)
            dve.tensor_scalar(veps[:, :], mv[:, :, 1], EPS, None, ALU.add).then_inc(Z["ln_std_in"], 1)
            dve.wait_ge(Z["w_hi_ready"], 3)
            dve.tensor_tensor(w_lo[:, 0:3, :], ps_m[:, 0:3 * D].rearrange("p (t n) -> p t n", t=3), raw(w_hi[:, 0:3, :]),
                              ALU.subtract).then_inc(Z["w_lo_ready"], 1)
            dve.tensor_tensor(w_lo[:, 3:5, :], w_raw[:, 4:6, :], raw(w_hi[:, 3:5, :]), ALU.subtract).then_inc(Z["w_lo_ready"], 1)
            dve.wait_ge(Z["std_ready"], 1)
            link("ln", dve.reciprocal(rstd[:, :], std[:, :]))
            link("ln", dve.tensor_tensor(newton[:, :], rstd[:, :], rstd[:, :], ALU.mult))
            link("ln", dve.tensor_tensor(newton[:, :], newton[:, :], veps[:, :], ALU.mult))
            link("ln", dve.tensor_scalar(newton[:, :], newton[:, :], -0.5, 1.5, ALU.mult, ALU.add))
            link("ln", dve.tensor_tensor(rstd[:, :], rstd[:, :], newton[:, :], ALU.mult))

            xh = raw(xnT_hi[:, :]).rearrange("e (p j) -> e j p", j=NT)
            xl = xnT_lo[:, :].rearrange("e (p j) -> e j p", j=NT)

            def normalise(r):
                if r >= 2:
                    dve.wait_ge(Z["xT_done"], r - 1)
                for j in range(TB * r, TB * (r + 1)):
                    dve.tensor_scalar(xn[:, r % 2, j % TB, :], x_sb[:, j, :], mv[:, j, 0:1], rstd[:, j:j + 1],
                                      ALU.subtract, ALU.mult).then_inc(Z["xn_ready"], 1)

            def xT_low(r):
                dve.wait_ge(Z["xT_hi"], r + 1)
                dve.tensor_tensor(xl[:, TB * r:TB * (r + 1), :], ps_t[:, r % 2, :].rearrange("e (j p) -> e j p", p=P),
                                  xh[:, TB * r:TB * (r + 1), :], ALU.subtract).then_inc(Z["xT_lo"], 1)

            normalise(0)
            normalise(1)
            for r in range(NR):
                xT_low(r)
                if r + 2 < NR:
                    normalise(r + 2)
            for r in range(NR):
                dve.wait_ge(Z["v_hi_ready"], r + 1)
                dve.tensor_tensor(v_lo[:, TB * r:TB * (r + 1), :], ps_s[:, r % 2, :].rearrange("p (j d) -> p j d", d=D),
                                  raw(v_hi[:, TB * r:TB * (r + 1), :]), ALU.subtract).then_inc(Z["v_lo_ready"], 1)
                dve.wait_ge(Z["rows_done"], r + 1)
                dve.wait_ge(Z["b_loaded"], 16 * 7)
                dve.tensor_tensor(t_rows[:, TB * r:TB * (r + 1), :], ps_s[:, 2 + r % 2, :].rearrange("p (j d) -> p j d", d=D),
                                  bsum[:, 2:3, :].to_broadcast([P, TB, D]), ALU.add).then_inc(Z["rows_ready"], 1)

            def q_low(n):
                dve.wait_ge(Z["q_hi_ready"], n)
                dve.scalar_tensor_tensor(out=q_lo[:, :], in0=ps_m[:, :], scalar=SCALE, in1=raw(q_hi[:, :]),
                                         op0=ALU.mult, op1=ALU.subtract).then_inc(Z["q_lo_ready"], 1)

            def step(it, c, scores=True, tr=True):
                i = it * TB + c
                if scores:
                    for b in range(NR):
                        dve.wait_ge(Z["scores_done"], i * NR + (b + 1))
                        dve.tensor_reduce(bank_max[:, c % 2, b:b + 1], ps_s[:, b, :], AX.X, ALU.max).then_inc(Z["part_max"], 1)
                    dve.wait_ge(Z["part_max"], (i + 1) * NR)
                    dve.tensor_reduce(neg_max[:, c % 2:c % 2 + 1], bank_max[:, c % 2, :], AX.X, ALU.max,
                                      negate=True).then_inc(Z["neg_max_ready"], 1)
                if tr:
                    for b in range(NR):
                        G = (c - 1) // 2 % 2
                        at = (slice(None), G, slice(TB * b, TB * (b + 1)), slice(P * ((c - 1) % 2), P * ((c - 1) % 2 + 1)))
                        dve.wait_ge(Z["pt_hi_ready"], (i - 1) * NR + (b + 1))
                        dve.tensor_tensor(pt_lo[at], ps_t[:, b % 2, :].rearrange("k (c q) -> k c q", q=P),
                                          raw(pt_hi[at]), ALU.subtract).then_inc(Z["pt_lo_ready"], 1)

            def bc_e(t):
                return t[:, :].unsqueeze(2).to_broadcast([P, NT, NE])

            def pick_first(one):
                link("route", dve.tensor_tensor(eq[:, :, :], eq[:, :, :], desc[:, :].unsqueeze(1).to_broadcast([P, NT, NE]), ALU.mult))
                link("route", dve.tensor_reduce(pick[:, :], eq[:, :, :], AX.X, ALU.max))
                link("route", dve.tensor_tensor(one[:, :, :], eq[:, :, :], bc_e(pick), ALU.is_equal))

            def route_choice():
                dve.wait_ge(Z["logits_done"], 1)
                dve.wait_ge(Z["consts"], 9)
                link("route", dve.tensor_tensor(lg[:, :, :], ps_o[:, 0:NT * NE].rearrange("p (j e) -> p j e", e=NE),
                                                bg_sb[:, :].unsqueeze(1).to_broadcast([P, NT, NE]), ALU.add))
                link("route", dve.tensor_reduce(top1[:, :], lg[:, :, :], AX.X, ALU.max))
                link("route", dve.tensor_tensor(eq[:, :, :], lg[:, :, :], bc_e(top1), ALU.is_equal))
                pick_first(one1)
                link("route", dve.scalar_tensor_tensor(out=lg[:, :, :], in0=one1[:, :, :], scalar=LOWEST, in1=lg[:, :, :],
                                                       op0=ALU.mult, op1=ALU.add))
                link("route", dve.tensor_reduce(top2[:, :], lg[:, :, :], AX.X, ALU.max))
                dve.tensor_tensor(gap[:, :], top2[:, :], top1[:, :], ALU.subtract).then_inc(Z["gap_ready"], 1)
                link("route", dve.tensor_tensor(eq[:, :, :], lg[:, :, :], bc_e(top2), ALU.is_equal))
                pick_first(one2)
                dve.tensor_tensor(both[:, :, :], one1[:, :, :], one2[:, :, :], ALU.add).then_inc(Z["both_ready"], 1)

            def route_gates():
                dve.wait_ge(Z["e2_ready"], 1)
                link("route", dve.tensor_scalar(den[:, :], e2[:, :], 1.0, None, ALU.add))
                link("route", dve.reciprocal(gate1[:, :], den[:, :]))
                link("route", dve.tensor_tensor(gate2[:, :], e2[:, :], gate1[:, :], ALU.mult))

            def route_slots():
                dve.wait_ge(Z["prefix_done"], 1)
                before = ps_o[:, BK // 4:BK // 4 + NT * NE].rearrange("p (j e) -> p j e", e=NE)
                totals = ps_o[:, BK // 2:BK // 2 + NT * NE].rearrange("p (j e) -> p e j", e=NE)
                link("route", dve.tensor_copy(tot[:, :, :], totals))
                flat = "p e j -> p (e j)"
                link("route", dve.tensor_tensor_scan(cum[:, :, :].rearrange(flat), first_tile[:, :, :].rearrange(flat),
                                                     tot[:, :, :].rearrange(flat), 0.0, ALU.mult, ALU.add))
                link("route", dve.tensor_tensor(eq[:, :, :].rearrange("p j e -> p (j e)").rearrange("p (e k) -> p e k", e=NE),
                                                cum[:, :, NT - 1:NT].to_broadcast([P, NE, NT]),
                                                thr[:, :].unsqueeze(1).to_broadcast([P, NE, NT]), ALU.is_gt))
                link("route", dve.tensor_reduce(tiles_e[:, :], eq[:, :, :].rearrange("p j e -> p (j e)").rearrange("p (e k) -> p e k", e=NE),
                                                AX.X, ALU.add))
                link("route", dve.tensor_tensor_scan(tiles_c[:, :], ones[:, 0:NE], tiles_e[:, :], 0.0, ALU.mult, ALU.add))
                link("route", dve.tensor_tensor(cmp[:, :, :], tile_no[:, :].unsqueeze(2).to_broadcast([P, MT, NE]),
                                                tiles_c[:, :].unsqueeze(1).to_broadcast([P, MT, NE]), ALU.is_ge))
                link("route", dve.tensor_reduce(texp_f[:, :], cmp[:, :, :], AX.X, ALU.add))
                dve.tensor_scalar(texp[:, :], texp_f[:, :], float(NE - 1), None, ALU.min).then_inc(Z["slots_ready"], 1)
                link("route", dve.tensor_tensor(tiles_x[:, :], tiles_c[:, :], tiles_e[:, :], ALU.subtract))
                link("route", dve.tensor_tensor(cum[:, :, :], cum[:, :, :], tot[:, :, :], ALU.subtract))
                link("route", dve.scalar_tensor_tensor(out=cum[:, :, :], in0=tiles_x[:, :].unsqueeze(2).to_broadcast([P, NE, NT]),
                                                       scalar=float(P), in1=cum[:, :, :], op0=ALU.mult, op1=ALU.add))
                link("route", dve.tensor_tensor(lg[:, :, :], before, cum[:, :, :].rearrange("p e j -> p j e"), ALU.add))
                link("route", dve.tensor_tensor(eq[:, :, :], lg[:, :, :], one1[:, :, :], ALU.mult))
                link("route", dve.tensor_reduce(pick[:, :], eq[:, :, :], AX.X, ALU.add))
                dve.tensor_copy(slot1[:, :], pick[:, :])
                link("route", dve.tensor_tensor(eq[:, :, :], lg[:, :, :], one2[:, :, :], ALU.mult))
                link("route", dve.tensor_reduce(top1[:, :], eq[:, :, :], AX.X, ALU.add))
                dve.tensor_copy(slot2[:, :], top1[:, :]).then_inc(Z["slots_ready"], 1)

            q_low(1)
            step(0, 0, tr=False)
            route_choice()
            step(0, 1)
            route_slots()
            step(0, 2)
            route_gates()
            q_low(2)
            step(0, 3)
            step(0, 4)
            step(0, 5)
            step(0, 6)

            def xgT_low(b):
                dve.wait_ge(Z["xgT_hi_ready"], b + 1)
                dve.tensor_tensor(xgT_lo[:, :], ps_m[:, :], raw(xgT_hi[:, :]), ALU.subtract).then_inc(Z["xgT_lo_ready"], 1)

            def l1_copy(b, u):
                i = b * TB + u
                dve.wait_ge(Z["l1_done"], i + 1)
                if not (exact(b) and i < 2):
                    dve.wait_ge(Z["midT_done"], i - 1)
                dve.tensor_copy(mid[:, u % 2, :], ps_s[:, u % 2, :]).then_inc(Z["l1_copied"], 1)

            def y_add(b, u):
                i = b * TB + u
                h = (u - 2) % TB // 2
                e = dve.value_load(texp[0:1, bass.ds(i - 2, 1)], min_val=0, max_val=NE - 1)
                dve.wait_ge(Z["y_done"], i - 1)
                if u % 2 == 0 and not (exact(b) and i < 6):
                    dve.wait_ge(s_y[h], b * 16 if h == 0 else (b - 1) * 16)
                dve.tensor_tensor(y_sb[:, (u - 2) % TB, :], ps_s[:, 2 + u % 2, 0:D], b2_sb[:, bass.ds(e, 1), :].rearrange("p a d -> p (a d)"),
                                  ALU.add).then_inc(Z["y_ready"], 1)

            def moe_batch(b, last=False):
                for u in range(TB):
                    l1_copy(b, u)
                    if u == TB - 1 and not last:
                        xgT_low(b + 1)
                    if not (exact(b) and b == 0 and u < 2):
                        y_add(b, u)

            dve.wait_ge(Z["w1_split"], NE)
            xgT_low(0)
            moe_batch(0)
            moe_batch(1)
            with dve.Fori(2, MB - 1) as b:
                moe_batch(b)
            moe_batch(MB - 1, last=True)
            y_add(MB, 0)
            y_add(MB, 1)

            def combine(j, zb, k):
                dve.wait_ge(s_z[zb], k * 32 + 32)
                dve.tensor_scalar(moe[:, bass.ds(j, 1), :].rearrange("p a d -> p (a d)"), z[:, zb, 0, :],
                                  gate1[:, bass.ds(j, 1)], None, ALU.mult).then_inc(Z["moe_link"], 1)
                dve.wait_ge(Z["moe_link"], j + 1)
                dve.scalar_tensor_tensor(out=moe[:, bass.ds(j, 1), :].rearrange("p a d -> p (a d)"), in0=z[:, zb, 1, :],
                                         scalar=gate2[:, bass.ds(j, 1)],
                                         in1=moe[:, bass.ds(j, 1), :].rearrange("p a d -> p (a d)"),
                                         op0=ALU.mult, op1=ALU.add).then_inc(Z["combined"], 1)

            with dve.Fori(1, NR - 1) as it:
                q_low(it + 2)
                for n in range(TB):
                    step(it, 3 + n)
                    for t in range(2):
                        combine(it * ZB + (2 * n + t - ZB), 2 * n + t, it - 1)
            step(NR - 1, 3)
            step(NR - 1, 4, scores=False)
            link("sums", dve.tensor_reduce(rinv[:, :], sums[:, :].rearrange("p (j b) -> p j b", b=NR), AX.X, ALU.add))
            link("sums", dve.reciprocal(rinv[:, :], rinv[:, :]))
            for r in range(NR):
                dve.wait_ge(Z["moeT_hi_ready"], r + 1)
                dve.tensor_tensor(moeT_view(moeT_lo, r), moeT_bank(r), raw(moeT_view(moeT_hi, r)),
                                  ALU.subtract).then_inc(Z["moeT_lo_ready"], 1)
            for r in range(NR):
                dve.wait_ge(Z["oTT_done"], r + 1)
                if r >= 2:
                    dve.wait_ge(Z["o_hi_ready"], r - 1)
                dve.tensor_tensor(o_sb[:, r % 2, :, :], ps_t[:, r % 2, :].rearrange("q (j d) -> q j d", d=D),
                                  rinv[:, TB * r:TB * (r + 1)].unsqueeze(2).to_broadcast([P, TB, D]),
                                  ALU.mult).then_inc(Z["o_ready"], 1)
                dve.wait_ge(Z["o_hi_ready"], r + 1)
                dve.tensor_tensor(o_lo[:, r % 2, :, :], o_sb[:, r % 2, :, :], raw(o_hi[:, r % 2, :, :]),
                                  ALU.subtract).then_inc(Z["o_lo_ready"], 1)
            dve.wait_ge(Z["x_biased"], 2)
            for r in range(NR):
                dve.wait_ge(Z["out_done"], r + 1)
                dve.tensor_tensor(x_sb[:, TB * r:TB * (r + 1), :], ps_s[:, r, :].rearrange("p (j e) -> p j e", e=D),
                                  x_sb[:, TB * r:TB * (r + 1), :], ALU.add).then_inc(Z["out_added"], 1)

        @block.tensor
        def _(pe):
            def product(dst, lhs, rhs, start=True, stop=True):
                (lh, ll), (rh, rl) = lhs, rhs
                pe.matmul(dst, lh, rh, start=start, stop=False)
                pe.matmul(dst, lh, rl, start=False, stop=False)
                return pe.matmul(dst, ll, rh, start=False, stop=stop)

            def w(n):
                return w_hi[:, n, :], w_lo[:, n, :]

            def xnT(cols):
                return xnT_hi[:, cols], xnT_lo[:, cols]

            pe.wait_ge(Z["consts"], 9)
            pe.wait_ge(Z["w_loaded"], 16 * 5)
            pe.matmul(ps_m[:, 0:D], w_raw[:, 0, :], w_raw[:, 1, :], start=True, stop=True)
            pe.transpose(ps_m[:, D:2 * D], w_raw[:, 2, :], ident[:, :])
            pe.transpose(ps_m[:, 3 * D:3 * D + NE * HC], b1_rows, ident[0:NE * HC, 0:NE * HC])
            pe.transpose(ps_m[:, 2 * D:3 * D], w_raw[:, 3, :], ident[:, :]).then_inc(Z["wT_done"], 1)

            for r in range(NR):
                pe.wait_ge(Z["xn_ready"], TB * (r + 1))
                if r >= 2:
                    pe.wait_ge(Z["xT_lo"], r - 1)
                for j in range(TB):
                    last = pe.transpose(ps_t[:, r % 2, P * j:P * (j + 1)], xn[:, r % 2, j, :], ident[:, :])
                last.then_inc(Z["xT_done"], 1)
            pe.wait_ge(Z["xT_lo"], NR)
            pe.wait_ge(Z["w_lo_ready"], 2)
            for r in range(NR):
                if r >= 2:
                    pe.wait_ge(Z["v_lo_ready"], r - 1)
                for j in range(TB):
                    last = product(ps_s[:, r % 2, D * j:D * (j + 1)], xnT(bass.ds((TB * r + j) * P, P)), w(WV))
                last.then_inc(Z["v_done"], 1)
                if r >= 2:
                    pe.wait_ge(Z["rows_ready"], r - 1)
                for j in range(TB):
                    last = product(ps_s[:, 2 + r % 2, D * j:D * (j + 1)], xnT(bass.ds((TB * r + j) * P, P)), w(WI))
                last.then_inc(Z["rows_done"], 1)
                if r >= 2:
                    pe.wait_ge(Z["tT_ready"], r - 1)
                product(tT_bank(r), w(WI), xnT(bass.ds(BK * r, BK))).then_inc(Z["tT_done"], 1)
            pe.wait_ge(Z["tT_ready"], NR)
            for j in range(NT):
                last = pe.matmul(ps_o[:, NE * j:NE * (j + 1)], tT[:, P * j:P * (j + 1)], wg_sb[:, :], start=True, stop=True)
            last.then_inc(Z["logits_done"], 1)

            def q_project(it):
                product(ps_m[:, :], w(MM), xnT(bass.ds(it * BK, BK))).then_inc(Z["q_done"], 1)

            def step(it, c, scores=True, tr=True, pv=True, q_next=None):
                i = it * TB + c
                if scores:
                    if c % TB == 0:
                        pe.wait_ge(Z["q_lo_ready"], it + (c // TB + 1))
                    for b in range(NR):
                        if not (exact(it) and i < 1):
                            pe.wait_ge(Z["exp_done"], (i - 1) * NR + (b + 1))
                        product(ps_s[:, b, :], (q_hi[:, P * (c % TB):P * (c % TB + 1)], q_lo[:, P * (c % TB):P * (c % TB + 1)]),
                                xnT(slice(BK * b, BK * (b + 1)))).then_inc(Z["scores_done"], 1)
                if q_next is not None:
                    q_project(q_next)
                g = it * 2 + ((c - 3) // 2)
                half = (c - 3) % 2
                for b in range(NR):
                    if tr:
                        pe.wait_ge(Z["exp_done"], (i - 1) * NR + (b + 1))
                        if not (exact(it) and i == 1 and b < 2):
                            pe.wait_ge(Z["pt_lo_ready"], (i - 1) * NR + (b - 1))
                        for k in range(TB):
                            at = BK * b + P * k
                            last = pe.transpose(ps_t[:, b % 2, P * k:P * (k + 1)], probs[:, at:at + P], ident[:, :])
                        last.then_inc(Z["pT_done"], 1)
                    if pv:
                        if b == 0 and half == 0:
                            pe.wait_ge(Z["pt_lo_ready"], (g + 1) * (2 * NR))
                            if not (exact(it) and it == 0 and c < 5):
                                pe.wait_ge(Z["oT_copied"], g)
                        G = (c - 3) // 2 % 2
                        for k in range(2):
                            ch = half * (NT // 2) + 2 * b + k
                            last = product(ps_o[:, 0:2 * P], (v_hi[:, ch, :], v_lo[:, ch, :]),
                                           (pt_hi[:, G, ch, :], pt_lo[:, G, ch, :]), start=(ch == 0), stop=(ch == NT - 1))
                        if ch == NT - 1:
                            last.then_inc(Z["pv_done"], 1)

            pe.wait_ge(Z["tT_ready"], NR)
            pe.wait_ge(Z["v_lo_ready"], NR)
            pe.wait_ge(Z["rows_ready"], NR)
            q_project(0)
            step(0, 0, tr=False, pv=False)
            step(0, 1, pv=False)
            pe.wait_ge(Z["both_ready"], 1)
            flat = both[:, :, :].rearrange("p j e -> p (j e)")
            pe.matmul(ps_o[:, BK // 4:BK // 4 + NT * NE], tri[:, :], flat, start=True, stop=True)
            pe.matmul(ps_o[:, BK // 2:BK // 2 + NT * NE], ones[:, :], flat, start=True, stop=True).then_inc(Z["prefix_done"], 1)
            step(0, 2, pv=False)
            pe.wait_ge(Z["slots_ready"], 2)
            step(0, 3, q_next=1)
            step(0, 4)
            step(0, 5)
            step(0, 6)

            def xg_transpose(b):
                pe.wait_ge(Z["xg_loaded"], (b + 1) * 16)
                if not (exact(b) and b == 0):
                    pe.wait_ge(Z["xgT_lo_ready"], b)
                for k in range(TB):
                    last = pe.transpose(ps_m[:, P * k:P * (k + 1)], xg[:, k, :], ident[:, :])
                last.then_inc(Z["xgT_done"], 1)

            def layer1(b, u):
                i = b * TB + u
                e = pe.value_load(texp[0:1, bass.ds(i, 1)], min_val=0, max_val=NE - 1)
                if u == 0:
                    pe.wait_ge(Z["xgT_lo_ready"], b + 1)
                if not (exact(b) and i < 2):
                    pe.wait_ge(Z["l1_copied"], i - 1)
                at = slice(P * u, P * (u + 1))
                w1e = [t[:, bass.ds(e, 1), :].rearrange("p a h -> p (a h)") for t in (w1_hi, w1_lo)]
                product(ps_s[:, u % 2, :], (xgT_hi[:, at], xgT_lo[:, at]), w1e).then_inc(Z["l1_done"], 1)

            def mid_transpose(b, u):
                i = b * TB + u
                pe.wait_ge(Z["l1_copied"], i)
                if not (exact(b) and i < 3):
                    pe.wait_ge(Z["midT_ready"], (i - 2) * HC)
                for k in range(HC):
                    last = pe.transpose(ps_t[:, (u - 1) % 2, P * k:P * (k + 1)], mid[:, (u - 1) % 2, P * k:P * (k + 1)], ident[:, :])
                last.then_inc(Z["midT_done"], 1)

            def layer2(b, u):
                i = b * TB + u
                e = pe.value_load(texp[0:1, bass.ds(i - 2, 1)], min_val=0, max_val=NE - 1)
                pe.wait_ge(Z["midT_ready"], (i - 1) * HC)
                if not (exact(b) and i < 4):
                    pe.wait_ge(Z["y_ready"], i - 3)
                for k in range(HC):
                    last = pe.matmul(ps_s[:, 2 + u % 2, 0:D], midT[:, u % 2, k, :],
                                     w2v[:, bass.ds(e, 1), k, :].rearrange("p a d -> p (a d)"),
                                     start=(k == 0), stop=(k == HC - 1))
                last.then_inc(Z["y_done"], 1)

            def moe_batch(b, last=False):
                for u in range(TB):
                    layer1(b, u)
                    if u == TB - 1 and not last:
                        xg_transpose(b + 1)
                    if not (exact(b) and b == 0 and u < 1):
                        mid_transpose(b, u)
                    if not (exact(b) and b == 0 and u < 2):
                        layer2(b, u)

            pe.wait_ge(Z["exp_done"], 7 * NR)
            pe.wait_ge(Z["pt_lo_ready"], 6 * NR)
            pe.wait_ge(Z["w1_split"], NE)
            pe.wait_ge(Z["w2_loaded"], 16)
            xg_transpose(0)
            moe_batch(0)
            with pe.Fori(1, MB - 1) as b:
                moe_batch(b)
            moe_batch(MB - 1, last=True)
            mid_transpose(MB, 0)
            layer2(MB, 0)
            layer2(MB, 1)
            pe.wait_ge(Z["l1_copied"], MT)
            pe.wait_ge(Z["y_ready"], MT)
            pe.wait_ge(Z["midT_ready"], MT * HC)

            with pe.Fori(1, NR - 1) as it:
                for n in range(TB):
                    step(it, 3 + n, q_next=it + 1 if n == 0 else None)
            step(NR - 1, 3)
            step(NR - 1, 4, scores=False)
            pe.wait_ge(Z["combined"], NT)
            for r in range(NR):
                pe.wait_ge(Z["exp_done"], NT * NR)
                for k in range(TB):
                    last = pe.transpose(ps_s[:, r, P * k:P * (k + 1)], moe[:, TB * r + k, :], ident[:, :])
                last.then_inc(Z["moeT_done"], 1)
            step(NR - 1, 5, scores=False, tr=False)
            step(NR - 1, 6, scores=False, tr=False)
            pe.wait_ge(Z["oT_copied"], NT // 2)
            pe.wait_ge(Z["moeT_lo_ready"], NR)

            def o_transpose(r):
                if r >= 2:
                    pe.wait_ge(Z["o_ready"], r - 1)
                for k in range(TB):
                    last = pe.transpose(ps_t[:, r % 2, P * k:P * (k + 1)], oT_all[:, TB * r + k, :], ident[:, :])
                last.then_inc(Z["oTT_done"], 1)
            o_transpose(0)
            o_transpose(1)
            for r in range(NR):
                for k in range(TB):
                    at = slice(P * (TB * r + k), P * (TB * r + k + 1))
                    product(ps_s[:, r, P * k:P * (k + 1)], (moeT_hi[:, at], moeT_lo[:, at]), w(WO), stop=False)
                    if k == 0:
                        pe.wait_ge(Z["o_lo_ready"], r + 1)
                    last = product(ps_s[:, r, P * k:P * (k + 1)], (o_hi[:, r % 2, k, :], o_lo[:, r % 2, k, :]), w(WP), start=False)
                last.then_inc(Z["out_done"], 1)
                if r + 2 < NR:
                    o_transpose(r + 2)


_INS = ['L0_attn_x', 'L0_attn_w_qkv', 'L0_attn_w_proj', 'L0_attn_b_proj', 'L0_ffn_W_in', 'L0_ffn_b_in',
        'L0_ffn_W_gate', 'L0_ffn_b_gate', 'L0_ffn_W1', 'L0_ffn_b1', 'L0_ffn_W2', 'L0_ffn_b2', 'L0_ffn_W_out',
        'L0_ffn_b_out']
_OUTS = [((1, 2048, 128), 'float32')]


def kernel(**inputs):
    import numpy as _np
    import concourse.bacc as _bacc
    from concourse import mybir as _mybir
    from concourse.bass_utils import run_bass_kernel_spmd as _run

    nc = _bacc.Bacc("TRN2", target_bir_lowering=False, num_devices=1)
    arrays, args = {}, []
    for name in _INS:
        a = _np.ascontiguousarray(inputs[name])
        arrays[f"in_{name}_dram"] = a
        args.append(nc.dram_tensor(f"in_{name}_dram", a.shape, _mybir.dt.from_np(a.dtype), kind="ExternalInput").ap())
    for i, (shape, dtype) in enumerate(_OUTS):
        dt = _mybir.dt.from_np(_np.dtype(dtype))
        args.append(nc.dram_tensor(f"out_{i}_dram", shape, dt, kind="ExternalOutput").ap())
    attention_moe_kernel(nc, *args)
    r = _run(nc, [arrays], core_ids=[0])
    return r.results[0]["out_0_dram"]
```

```python
import concourse.bass as bass
from concourse import mybir
from contextlib import ExitStack

FP32 = mybir.dt.float32
FP32R = mybir.dt.float32r
I32 = mybir.dt.int32
U32 = mybir.dt.uint32
ALU = mybir.AluOpType
ACT = mybir.ActivationFunctionType
AX = mybir.AxisListType


def attention_moe_kernel(nc, x, w_qkv, w_proj, b_proj, w_in, b_in, w_gate, b_gate,
                         w1, b1, w2, b2, w_out, b_out, out):
    P = 128
    S, D = x.shape[1], x.shape[2]
    NT = S // P
    NE, _, DM = w1.shape
    HC = DM // P
    BK = 512
    NR = S // BK
    TB = BK // P
    TOPK = 2
    MT = -(-(TOPK * NT + NE - 1) // TB) * TB
    MB = MT // TB
    HEADS = 16
    SCALE = 1.0 / float(D // HEADS) ** 0.5
    EPS = 1e-5
    LOWEST = -3.0e38

    ctx = ExitStack()
    with ctx:
        def sb(name, shape, dt=FP32):
            return ctx.enter_context(nc.sbuf_tensor(name, shape, dt))

        def sem(name):
            return ctx.enter_context(nc.semaphore(name))

        slots_in = nc.dram_tensor("slots_in", (MT * P, D), FP32, kind="Internal").ap()
        slots_out = nc.dram_tensor("slots_out", (MT * P, D), FP32, kind="Internal").ap()

        x_sb = sb("x_sb", [P, NT, D])
        xnT_hi = sb("xnT_hi", [P, S], FP32R)
        xnT_lo = sb("xnT_lo", [P, S], FP32R)
        v_hi = sb("v_hi", [P, NT, D], FP32R)
        v_lo = sb("v_lo", [P, NT, D], FP32R)
        q_hi = sb("q_hi", [P, BK], FP32R)
        q_lo = sb("q_lo", [P, BK], FP32R)
        probs = sb("probs", [P, S])
        pt_hi = sb("pt_hi", [P, 2, NT, 2 * P], FP32R)
        pt_lo = sb("pt_lo", [P, 2, NT, 2 * P], FP32R)
        oT_all = sb("oT_all", [P, NT, P])
        w1_hi = sb("w1_hi", [P, NE, DM], FP32R)
        w1_lo = sb("w1_lo", [P, NE, DM], FP32R)
        w2_sb = sb("w2_sb", [P, NE * HC * D])
        w1_raw = sb("w1_raw", [P, 2, DM])
        mm_hi = sb("mm_hi", [P, D], FP32R)
        mm_lo = sb("mm_lo", [P, D], FP32R)
        vt_hi = sb("vt_hi", [P, 2, D], FP32R)
        vt_lo = sb("vt_lo", [P, 2, D], FP32R)
        gate_w = sb("gate_w", [P, 2, NE], FP32R)
        wpT = sb("wpT", [P, D])
        wo_sb = sb("wo_sb", [P, D])
        ident = sb("ident", [P, P])
        tri = sb("tri", [P, P])
        ones = sb("ones", [P, P])
        bsum = sb("bsum", [P, 3, D])
        bin_col = sb("bin_col", [P, 1])
        wg_sb = sb("wg_sb", [P, NE])
        bg_sb = sb("bg_sb", [P, NE])
        b1_col = sb("b1_col", [P, NE, HC])
        b2_sb = sb("b2_sb", [P, NE, D])
        stats = sb("stats", [P, NT, 6])
        mv = sb("mv", [P, NT, 2])
        veps = sb("veps", [P, NT])
        std = sb("std", [P, NT])
        rstd = sb("rstd", [P, NT])
        newton = sb("newton", [P, NT])
        nmr = sb("nmr", [P, NT])
        gate_b = sb("gate_b", [P, NE])
        bank_max = sb("bank_max", [P, 2, NR])
        neg_max = sb("neg_max", [P, 2])
        sums = sb("sums", [P, NT * NR])
        rinv = sb("rinv", [P, NT])
        lg = sb("lg", [P, NT, NE])
        eq = sb("eq", [P, NT, NE])
        one1 = sb("one1", [P, NT, NE])
        one2 = sb("one2", [P, NT, NE])
        both = sb("both", [P, NT, NE])
        desc = sb("desc", [P, NE])
        first_tile = sb("first_tile", [P, NE, NT])
        tot = sb("tot", [P, NE, NT])
        cum = sb("cum", [P, NE, NT])
        thr = sb("thr", [P, NT])
        tiles_e = sb("tiles_e", [P, NE])
        tiles_c = sb("tiles_c", [P, NE])
        tiles_x = sb("tiles_x", [P, NE])
        tile_no = sb("tile_no", [P, MT])
        cmp = sb("cmp", [P, MT, NE])
        texp_f = sb("texp_f", [P, MT])
        texp = sb("texp", [P, MT], I32)
        top1 = sb("top1", [P, NT])
        top2 = sb("top2", [P, NT])
        pick = sb("pick", [P, NT])
        gap = sb("gap", [P, NT])
        e2 = sb("e2", [P, NT])
        den = sb("den", [P, NT])
        gate1 = sb("gate1", [P, NT])
        gate2 = sb("gate2", [P, NT])
        slot1 = sb("slot1", [P, NT], I32)
        slot2 = sb("slot2", [P, NT], I32)
        xgT_hi = sb("xgT_hi", [P, BK], FP32R)
        xgT_lo = sb("xgT_lo", [P, BK], FP32R)
        mid = sb("mid", [P, 2, DM])
        xn = probs[:, 0:2 * BK].rearrange("p (b j e) -> p b j e", b=2, e=D)
        xg = w1_raw[:, 0, :].rearrange("p (j d) -> p j d", d=D)
        y_sb = w1_raw[:, 1, :].rearrange("p (j d) -> p j d", d=D)
        w_raw = w2_sb[:, 0:5 * D].rearrange("p (t e) -> p t e", e=D)
        winT = w2_sb[:, 5 * D:6 * D]
        bin_rows = w2_sb[:, 6 * D:7 * D]
        t_rows = w2_sb[:, S:2 * S].rearrange("p (j d) -> p j d", d=D)
        w2v = w2_sb[:, :].rearrange("p (e c d) -> p e c d", e=NE, d=D)
        ZB = 8
        moe = w2_sb[:, 0:S].rearrange("p (j d) -> p j d", d=D)
        z = w2_sb[:, S:2 * S].rearrange("p (b t d) -> p b t d", b=ZB, d=D)
        o_sb = mid[:, :, :].rearrange("p b (j d) -> p b j d", d=D)
        moeT = w2_sb[:, S:2 * S]

        midT = oT_all[:, NT // 2:NT, :].rearrange("p (b c) n -> p b c n", b=2)

        b1_rows = mid[0:NE * HC, 0, 0:P]

        def raw(ap):
            return ap.bitcast(FP32)

        ps_s = ctx.enter_context(nc.psum_tensor("ps_s", [P, NR, BK], FP32))
        ps_t = ctx.enter_context(nc.psum_tensor("ps_t", [P, 2, BK], FP32))
        ps_o = ctx.enter_context(nc.psum_tensor("ps_o", [P, BK], FP32))
        ps_m = ctx.enter_context(nc.psum_tensor("ps_m", [P, BK], FP32))

        Z = {n: sem(n) for n in """
            w_loaded b_loaded consts zero_ready zeroed ln_link ln_std_in std_ready ln_ready xn_ready
            xT_done xT_hi xT_lo wT_done w_hi_ready w_lo_ready winT_ready gate_done gate_ready x_biased
            vt_done v_hi_ready v_lo_ready rows_ready logits_done
            q_done q_hi_ready q_lo_ready scores_done part_max neg_max_ready exp_done
            pT_done pt_hi_ready pt_lo_ready pv_done oT_copied
            route_link gap_ready e2_ready both_ready prefix_done slots_ready scattered
            w1_split w2_loaded xn_act_ready ln_bias_ready w1_hi_ready
            xg_loaded xgT_done xgT_hi_ready xgT_lo_ready l1_done l1_copied midT_done midT_ready
            y_done y_ready combined moe_link moeT_done moeT_ready
            sums_link rinv_ready oTT_done o_ready out_done out_added stored
            """.split()}
        s_x = [sem(f"x_loaded{r}") for r in range(NR)]
        s_w1 = [sem(f"w1_loaded{r}") for r in range(2)]
        s_y = [sem(f"y_stored{r}") for r in range(2)]
        s_z = [sem(f"z_loaded{r}") for r in range(ZB)]

        def expert_of(eng, first, n):
            _, values = nc.values_load_multi_w_load_instructions(
                texp[0:1, bass.ds(first, n)], engines=[eng.engine], min_val=0, max_val=NE - 1,
                skip_runtime_bounds_check_because="a count of experts that is clamped to the last one")
            return list(values)

        def exact(it):
            return isinstance(it, int)

        def vt_bank(n):
            return ps_s[:, n % NR, :].rearrange("p (j t d) -> p j t d", j=2, t=2)

        def moeT_view(r):
            return moeT.rearrange("d (j p) -> d p j", p=P)[:, 32 * r:32 * (r + 1), :]

        def moeT_bank(r):
            return ps_s[:, r, :].rearrange("d (p j) -> d p j", j=NT)

        block = ctx.enter_context(nc.Block())

        @block.sync
        def _(sp):
            xv = x.rearrange("o (p j) e -> p (o j) e", p=P)
            for r in range(NR):
                sp.dma_start(x_sb[:, TB * r:TB * (r + 1), :], xv[:, TB * r:TB * (r + 1), :]).then_inc(s_x[r], 16)
            sp.wait_ge(Z["w_loaded"], 16 * 7)
            sp.wait_ge(Z["zero_ready"], 1)
            zero = pt_hi[:, 0, :, :].rearrange("p a b -> p (a b)").bitcast(FP32)
            zv = slots_in.rearrange("(b p r) d -> b p (r d)", p=P, b=2)
            for b in range(2):
                sp.dma_start(zv[b], zero[:, 0:MT // 2 * D]).then_inc(Z["zeroed"], 16)
            for e in range(NE):
                if e >= 2:
                    sp.wait_ge(Z["w1_split"], e - 1)
                sp.dma_start(w1_raw[:, e % 2, :], w1[e]).then_inc(s_w1[e % 2], 16)
            w2_src = w2.rearrange("e (c p) d -> p e c d", p=P)
            sp.wait_ge(Z["w_lo_ready"], 2)
            sp.wait_ge(Z["gate_done"], 1)
            sp.dma_start(w2v[:, 0:NE // 2], w2_src[:, 0:NE // 2]).then_inc(Z["w2_loaded"], 16)

            xg_src = slots_in.rearrange("(t p) d -> p t d", p=P)
            y_dst = slots_out.rearrange("(t p) d -> p t d", p=P)

            def load_xg(b):
                sp.dma_start(xg[:, :, :], xg_src[:, bass.ds(b * TB, TB), :]).then_inc(Z["xg_loaded"], 16)

            def store_y(b, h):
                sp.wait_ge(Z["y_ready"], b * TB + (2 * h + 2))
                sp.dma_start(y_dst[:, bass.ds(b * TB + 2 * h, 2), :], y_sb[:, 2 * h:2 * h + 2, :]).then_inc(s_y[h], 16)

            sp.wait_ge(Z["scattered"], 16 * TOPK * NT)
            sp.wait_ge(Z["w1_split"], NE)
            sp.dma_start(w2v[:, NE // 2:NE], w2_src[:, NE // 2:NE]).then_inc(Z["w2_loaded"], 16)
            load_xg(0)
            sp.wait_ge(Z["xgT_done"], 1)
            load_xg(1)
            with sp.Fori(0, MB - 2) as b:
                store_y(b, 0)
                sp.wait_ge(Z["xgT_done"], b + 2)
                load_xg(b + 2)
                store_y(b, 1)
            for b in range(MB - 2, MB):
                store_y(b, 0)
                store_y(b, 1)
            ov = out.rearrange("o (p j) e -> p (o j) e", p=P)
            for r in range(NR):
                sp.wait_ge(Z["out_added"], r + 1)
                sp.dma_start(ov[:, TB * r:TB * (r + 1), :], x_sb[:, TB * r:TB * (r + 1), :]).then_inc(Z["stored"], 16)
            sp.wait_ge(Z["stored"], 16 * NR)

        @block.gpsimd
        def _(pool):
            pool.memset(raw(pt_hi[:, 0, :, :]), 0.0).then_inc(Z["zero_ready"], 1)
            pool.memset(ident[:, :], 0.0).then_inc(Z["consts"], 1)
            pool.memset(ones[:, :], 1.0).then_inc(Z["consts"], 1)
            pool.memset(first_tile[:, :, :], 1.0).then_inc(Z["consts"], 1)
            pool.iota(desc[:, :], pattern=[[-1, NE]], base=NE, channel_multiplier=0,
                      allow_small_or_imprecise_dtypes=True).then_inc(Z["consts"], 1)
            pool.iota(thr[:, :], pattern=[[P, NT]], base=0, channel_multiplier=0,
                      allow_small_or_imprecise_dtypes=True).then_inc(Z["consts"], 1)
            pool.iota(tile_no[:, :], pattern=[[1, MT]], base=0, channel_multiplier=0,
                      allow_small_or_imprecise_dtypes=True).then_inc(Z["consts"], 1)
            pool.wait_ge(Z["consts"], 6)
            pool.affine_select(out=ident[:, :], in_=ident[:, :], compare_op=ALU.not_equal, fill=1.0,
                               base=0, pattern=[[-1, P]], channel_multiplier=1).then_inc(Z["consts"], 1)
            pool.affine_select(out=tri[:, :], in_=ones[:, :], compare_op=ALU.is_gt, fill=0.0,
                               base=0, pattern=[[1, P]], channel_multiplier=-1).then_inc(Z["consts"], 1)
            pool.affine_select(out=first_tile[:, :, :], in_=first_tile[:, :, :], compare_op=ALU.is_gt, fill=0.0,
                               base=0, pattern=[[0, NE], [1, NT]], channel_multiplier=0).then_inc(Z["consts"], 1)
            for e in range(NE):
                pool.wait_ge(s_w1[e % 2], 16 * (e // 2 + 1))
                pool.tensor_copy(w1_hi[:, e, :], w1_raw[:, e % 2, :]).then_inc(Z["w1_hi_ready"], 1)
                pool.wait_ge(Z["w1_hi_ready"], e + 1)
                pool.tensor_tensor(w1_lo[:, e, :], w1_raw[:, e % 2, :], raw(w1_hi[:, e, :]),
                                   ALU.subtract).then_inc(Z["w1_split"], 1)
            pool.wait_ge(Z["zeroed"], 32)
            pool.wait_ge(Z["slots_ready"], 2)
            pool.wait_ge(Z["rows_ready"], NT // 2)
            for j in range(NT):
                for s in (slot1, slot2):
                    pool.indirect_dma_start(out=slots_in, out_offset=bass.IndirectOffsetOnAxis(ap=s[:, j:j + 1], axis=0),
                                            in_=t_rows[:, j, :], in_offset=None).then_inc(Z["scattered"], 16)
            pool.wait_ge(Z["b_loaded"], 16 * 5)
            pool.wait_ge(Z["xn_ready"], NT // 2)
            pool.wait_ge(Z["xn_act_ready"], NT // 2)
            pool.tensor_tensor(bsum[:, 0, :], bsum[:, 0, :], bsum[:, 1, :], ALU.add).then_inc(Z["x_biased"], 1)
            pool.wait_ge(Z["x_biased"], 1)
            pool.tensor_tensor(x_sb[:, :, :], x_sb[:, :, :], bsum[:, 0:1, :].to_broadcast([P, NT, D]),
                               ALU.add).then_inc(Z["x_biased"], 1)
            for h in range(2):
                pool.wait_ge(s_y[h], 16 * MB)
            pool.wait_ge(Z["y_done"], MT)
            for j in range(NT):
                if j >= ZB:
                    pool.wait_ge(Z["combined"], j - ZB + 1)
                for t, s in enumerate((slot1, slot2)):
                    pool.indirect_dma_start(out=z[:, j % ZB, t, :], out_offset=None, in_=slots_out,
                                            in_offset=bass.IndirectOffsetOnAxis(ap=s[:, j:j + 1], axis=0)
                                            ).then_inc(s_z[j % ZB], 16)

        @block.scalar
        def _(act):
            wv_ = w_qkv.rearrange("(t p) e -> p t e", p=P)
            act.dma_start(w_raw[:, 0:3, :], wv_).then_inc(Z["w_loaded"], 16)
            act.dma_start(w_raw[:, 3, :], w_proj).then_inc(Z["w_loaded"], 16)
            act.dma_start(w_raw[:, 4, :], w_in).then_inc(Z["w_loaded"], 16)
            act.dma_start(wo_sb[:, :], w_out).then_inc(Z["w_loaded"], 16)
            act.dma_start(wg_sb[:, :], w_gate).then_inc(Z["w_loaded"], 16)
            act.dma_start(bin_col[:, :], b_in.rearrange("(p a) -> p a", a=1)).then_inc(Z["w_loaded"], 16)
            act.dma_start(b1_rows, b1.rearrange("e (c p) -> (e c) p", p=P)).then_inc(Z["w_loaded"], 16)

            def rows(v, n):
                return v.rearrange("(a n) -> a n", a=1).to_broadcast([P, n])
            act.dma_start(bsum[:, 0, :], rows(b_proj, D)).then_inc(Z["b_loaded"], 16)
            act.dma_start(bsum[:, 1, :], rows(b_out, D)).then_inc(Z["b_loaded"], 16)
            act.dma_start(bsum[:, 2, :], rows(b_in, D)).then_inc(Z["b_loaded"], 16)
            act.dma_start(bg_sb[:, :], rows(b_gate, NE)).then_inc(Z["b_loaded"], 16)
            act.dma_start(b2_sb[:, :, :].rearrange("p e d -> p (e d)"),
                          b2.rearrange("(a e) d -> a (e d)", a=1).to_broadcast([P, NE * D])).then_inc(Z["b_loaded"], 16)

            act.wait_ge(Z["ln_std_in"], 1)
            act.activation(std[:, :], veps[:, :], ACT.Sqrt).then_inc(Z["std_ready"], 1)
            act.wait_ge(Z["wT_done"], 1)
            act.activation(winT, ps_m[:, 2 * D:3 * D], ACT.Copy).then_inc(Z["winT_ready"], 1)
            act.activation(vt_hi[:, 0, :], ps_m[:, D:2 * D], ACT.Copy).then_inc(Z["w_hi_ready"], 1)
            act.activation(vt_hi[:, 1, :], w_raw[:, 4, :], ACT.Copy).then_inc(Z["w_hi_ready"], 1)
            act.activation(mm_hi[:, :], ps_m[:, 0:D], ACT.Copy).then_inc(Z["w_hi_ready"], 1)
            act.activation(b1_col[:, :, :].rearrange("p e c -> p (e c)"), ps_m[:, 3 * D:3 * D + NE * HC],
                           ACT.Copy).then_inc(Z["w_hi_ready"], 1)

            def normalise(r):
                if r >= 2:
                    act.wait_ge(Z["xT_done"], r - 1)
                for j in range(TB * r + 2, TB * (r + 1)):
                    act.activation(xn[:, r % 2, j % TB, :], x_sb[:, j, :], ACT.Identity, bias=nmr[:, j:j + 1],
                                   scale=rstd[:, j:j + 1]).then_inc(Z["xn_act_ready"], 1)

            xh = xnT_hi[:, :].rearrange("e (p j) -> e j p", j=NT)

            def xT_high(r):
                act.wait_ge(Z["xT_done"], r + 1)
                act.activation(xh[:, TB * r:TB * (r + 1), :], ps_t[:, r % 2, :].rearrange("e (j p) -> e j p", p=P),
                               ACT.Copy).then_inc(Z["xT_hi"], 1)

            def v_high(n):
                act.wait_ge(Z["vt_done"], n + 1)
                act.activation(v_hi[:, 2 * n:2 * n + 2, :], vt_bank(n)[:, :, 0, :], ACT.Copy).then_inc(Z["v_hi_ready"], 1)

            act.wait_ge(Z["ln_bias_ready"], 1)
            normalise(0)
            normalise(1)
            for r in range(NR):
                xT_high(r)
                if r == 0:
                    act.wait_ge(Z["gate_done"], 1)
                    act.activation(gate_w[:, 0, :], ps_o[:, D:D + NE], ACT.Copy).then_inc(Z["gate_ready"], 1)
                    act.activation(wpT[:, :], ps_o[:, 0:D], ACT.Copy).then_inc(Z["gate_ready"], 1)
                if r + 2 < NR:
                    normalise(r + 2)
            for n in range(NT // 2):
                v_high(n)

            def q_split(n):
                act.wait_ge(Z["q_done"], n)
                act.activation(q_hi[:, :], ps_m[:, :], ACT.Copy, scale=SCALE).then_inc(Z["q_hi_ready"], 1)

            def step(it, c, scores=True, tr=True):
                i = it * TB + c
                for b in range(NR):
                    if tr:
                        if b == 0 and (c - 1) % 2 == 0 and not (exact(it) and i < 5):
                            act.wait_ge(Z["pv_done"], it * 2 + ((c - 1) // 2 - 1))
                        act.wait_ge(Z["pT_done"], (i - 1) * NR + (b + 1))
                        act.activation(pt_hi[:, (c - 1) // 2 % 2, TB * b:TB * (b + 1), P * ((c - 1) % 2):P * ((c - 1) % 2 + 1)],
                                       ps_t[:, b % 2, :].rearrange("k (c q) -> k c q", q=P),
                                       ACT.Copy).then_inc(Z["pt_hi_ready"], 1)
                    if scores:
                        if b == 0:
                            act.wait_ge(Z["neg_max_ready"], i + 1)
                        act.activation(probs[:, BK * b:BK * (b + 1)], ps_s[:, b, :], ACT.Exp,
                                       bias=neg_max[:, c % 2:c % 2 + 1],
                                       accum_out=sums[:, bass.ds(i * NR + b, 1)]).then_inc(Z["exp_done"], 1)

            def copy_o(g):
                act.wait_ge(Z["pv_done"], g + 1)
                act.activation(oT_all[:, bass.ds(g * 2, 2), :], ps_o[:, 0:2 * P].rearrange("p (a b) -> p a b", a=2),
                               ACT.Copy).then_inc(Z["oT_copied"], 1)

            q_split(1)
            act.wait_ge(Z["zeroed"], 32)
            step(0, 0, tr=False)
            act.wait_ge(Z["gap_ready"], 1)
            act.activation(e2[:, :], gap[:, :], ACT.Exp).then_inc(Z["e2_ready"], 1)
            step(0, 1)
            step(0, 2)
            q_split(2)
            step(0, 3)
            step(0, 4)
            copy_o(0)
            step(0, 5)
            step(0, 6)
            copy_o(1)

            def xgT_split(b):
                act.wait_ge(Z["xgT_done"], b + 1)
                if not (exact(b) and b < 1):
                    act.wait_ge(Z["l1_done"], b * TB)
                act.activation(xgT_hi[:, :], ps_m[:, :], ACT.Copy).then_inc(Z["xgT_hi_ready"], 1)

            def moe_relu(b, u, e):
                i = b * TB + u
                act.wait_ge(Z["midT_done"], i)
                if not (exact(b) and i < 3):
                    act.wait_ge(Z["y_done"], i - 2)
                for c in range(HC):
                    act.activation(midT[:, (u - 1) % 2, c, :], ps_t[:, (u - 1) % 2, P * c:P * (c + 1)], ACT.Relu,
                                   bias=b1_col[:, bass.ds(e, 1), c]).then_inc(Z["midT_ready"], 1)

            xgT_split(0)
            act.wait_ge(Z["slots_ready"], 2)

            def moe_batch(b, last=False, start=0):
                experts = [None] * start + expert_of(act, b * TB - 1 + start, TB - start)
                for u in range(start, TB):
                    if u == TB - 1 and not last:
                        xgT_split(b + 1)
                    moe_relu(b, u, experts[u])
            moe_batch(0, start=1)
            with act.Fori(1, MB - 1) as b:
                moe_batch(b)
            moe_batch(MB - 1, last=True)
            moe_relu(MB, 0, expert_of(act, MT - 1, 1)[0])

            def attention_group(it):
                q_split(it + 2)
                step(it, 3)
                step(it, 4)
                copy_o(it * 2)
                step(it, 5)
                step(it, 6)
                copy_o(it * 2 + 1)

            with act.Fori(1, NR - 1) as it:
                attention_group(it)
            step(NR - 1, 3)
            step(NR - 1, 4, scores=False)
            copy_o(NT // 2 - 2)
            for r in range(NR):
                act.wait_ge(Z["moeT_done"], r + 1)
                act.activation(moeT_view(r), moeT_bank(r), ACT.Copy).then_inc(Z["moeT_ready"], 1)
            copy_o(NT // 2 - 1)

        @block.vector
        def _(dve):
            count = {"ln": 0, "route": 0, "moe": 0, "sums": 0}

            def link(key, inst):
                count[key] += 1
                s = Z[key + "_link"]
                inst.then_inc(s, 1)
                dve.wait_ge(s, count[key])

            for r in range(NR):
                dve.wait_ge(s_x[r], 16)
                for j in range(TB * r, TB * (r + 1)):
                    dve.bn_stats(stats[:, j, :], x_sb[:, j, :]).then_inc(Z["ln_link"], 1)
                if r > 0:
                    dve.wait_ge(Z["ln_link"], TB * r)
                    for j in range(TB * (r - 1), TB * r):
                        dve.bn_aggr(mv[:, j, :], stats[:, j, :])
            count["ln"] = NT
            dve.wait_ge(Z["ln_link"], NT)
            for j in range(NT - TB, NT):
                last = dve.bn_aggr(mv[:, j, :], stats[:, j, :])
            link("ln", last)
            link("ln", dve.tensor_scalar(veps[:, :], mv[:, :, 1], EPS, None, ALU.add))
            dve.tensor_scalar(newton[:, :], veps[:, :], -0.5, None, ALU.mult).then_inc(Z["ln_std_in"], 1)
            dve.wait_ge(Z["std_ready"], 1)
            link("ln", dve.reciprocal(rstd[:, :], std[:, :]))
            link("ln", dve.tensor_tensor(nmr[:, :], rstd[:, :], rstd[:, :], ALU.mult))
            link("ln", dve.tensor_tensor(newton[:, :], newton[:, :], nmr[:, :], ALU.mult))
            link("ln", dve.scalar_tensor_tensor(out=rstd[:, :], in0=newton[:, :], scalar=1.5, in1=rstd[:, :],
                                                op0=ALU.add, op1=ALU.mult))
            dve.scalar_tensor_tensor(out=nmr[:, :], in0=mv[:, :, 0], scalar=-1.0, in1=rstd[:, :],
                                     op0=ALU.mult, op1=ALU.mult).then_inc(Z["ln_bias_ready"], 1)

            xh = raw(xnT_hi[:, :]).rearrange("e (p j) -> e j p", j=NT)
            xl = xnT_lo[:, :].rearrange("e (p j) -> e j p", j=NT)

            def normalise(r):
                if r >= 2:
                    dve.wait_ge(Z["xT_done"], r - 1)
                for j in range(TB * r, TB * r + 2):
                    dve.tensor_scalar(xn[:, r % 2, j % TB, :], x_sb[:, j, :], mv[:, j, 0:1], rstd[:, j:j + 1],
                                      ALU.subtract, ALU.mult).then_inc(Z["xn_ready"], 1)

            def xT_low(r):
                dve.wait_ge(Z["xT_hi"], r + 1)
                dve.tensor_tensor(xl[:, TB * r:TB * (r + 1), :], ps_t[:, r % 2, :].rearrange("e (j p) -> e j p", p=P),
                                  xh[:, TB * r:TB * (r + 1), :], ALU.subtract).then_inc(Z["xT_lo"], 1)

            normalise(0)
            normalise(1)
            dve.wait_ge(Z["w_hi_ready"], 4)
            dve.tensor_tensor(vt_lo[:, 0, :], ps_m[:, D:2 * D], raw(vt_hi[:, 0, :]), ALU.subtract)
            dve.tensor_tensor(vt_lo[:, 1, :], w_raw[:, 4, :], raw(vt_hi[:, 1, :]), ALU.subtract).then_inc(Z["w_lo_ready"], 1)
            dve.tensor_tensor(mm_lo[:, :], ps_m[:, 0:D], raw(mm_hi[:, :]), ALU.subtract).then_inc(Z["w_lo_ready"], 1)
            for r in range(NR):
                xT_low(r)
                if r == 0:
                    dve.wait_ge(Z["gate_ready"], 2)
                    dve.wait_ge(Z["b_loaded"], 16 * 5)
                    dve.tensor_tensor(gate_w[:, 1, :], ps_o[:, D:D + NE], raw(gate_w[:, 0, :]), ALU.subtract)
                    dve.tensor_tensor(gate_b[:, :], ps_o[:, D + NE:D + 2 * NE], bg_sb[:, :], ALU.add).then_inc(Z["w_lo_ready"], 1)
                if r + 2 < NR:
                    normalise(r + 2)
            for n in range(NT // 2):
                dve.wait_ge(Z["v_hi_ready"], n + 1)
                dve.tensor_tensor(v_lo[:, 2 * n:2 * n + 2, :], vt_bank(n)[:, :, 0, :], raw(v_hi[:, 2 * n:2 * n + 2, :]),
                                  ALU.subtract).then_inc(Z["v_lo_ready"], 1)
                dve.tensor_tensor(t_rows[:, 2 * n:2 * n + 2, :], vt_bank(n)[:, :, 1, :],
                                  bsum[:, 2:3, :].to_broadcast([P, 2, D]), ALU.add).then_inc(Z["rows_ready"], 1)

            def q_low(n):
                dve.wait_ge(Z["q_hi_ready"], n)
                dve.scalar_tensor_tensor(out=q_lo[:, :], in0=ps_m[:, :], scalar=SCALE, in1=raw(q_hi[:, :]),
                                         op0=ALU.mult, op1=ALU.subtract).then_inc(Z["q_lo_ready"], 1)

            def step(it, c, scores=True, tr=True):
                i = it * TB + c
                if scores:
                    for b in range(NR):
                        dve.wait_ge(Z["scores_done"], i * NR + (b + 1))
                        dve.tensor_reduce(bank_max[:, c % 2, b:b + 1], ps_s[:, b, :], AX.X, ALU.max).then_inc(Z["part_max"], 1)
                    dve.wait_ge(Z["part_max"], (i + 1) * NR)
                    dve.tensor_reduce(neg_max[:, c % 2:c % 2 + 1], bank_max[:, c % 2, :], AX.X, ALU.max,
                                      negate=True).then_inc(Z["neg_max_ready"], 1)
                if tr:
                    for b in range(NR):
                        G = (c - 1) // 2 % 2
                        at = (slice(None), G, slice(TB * b, TB * (b + 1)), slice(P * ((c - 1) % 2), P * ((c - 1) % 2 + 1)))
                        dve.wait_ge(Z["pt_hi_ready"], (i - 1) * NR + (b + 1))
                        dve.tensor_tensor(pt_lo[at], ps_t[:, b % 2, :].rearrange("k (c q) -> k c q", q=P),
                                          raw(pt_hi[at]), ALU.subtract).then_inc(Z["pt_lo_ready"], 1)

            def bc_e(t):
                return t[:, :].unsqueeze(2).to_broadcast([P, NT, NE])

            def pick_first(one):
                link("route", dve.tensor_tensor(eq[:, :, :], eq[:, :, :], desc[:, :].unsqueeze(1).to_broadcast([P, NT, NE]), ALU.mult))
                link("route", dve.tensor_reduce(pick[:, :], eq[:, :, :], AX.X, ALU.max))
                link("route", dve.tensor_tensor(one[:, :, :], eq[:, :, :], bc_e(pick), ALU.is_equal))

            def route_choice():
                dve.wait_ge(Z["logits_done"], 1)
                dve.wait_ge(Z["consts"], 9)
                parts = ps_o[:, 0:2 * NT * NE].rearrange("p (j t e) -> p j t e", t=2, e=NE)
                link("route", dve.tensor_tensor(lg[:, :, :], parts[:, :, 1, :],
                                                gate_b[:, :].unsqueeze(1).to_broadcast([P, NT, NE]), ALU.add))
                link("route", dve.tensor_tensor(lg[:, :, :], parts[:, :, 0, :], lg[:, :, :], ALU.add))
                link("route", dve.tensor_reduce(top1[:, :], lg[:, :, :], AX.X, ALU.max))
                link("route", dve.tensor_tensor(eq[:, :, :], lg[:, :, :], bc_e(top1), ALU.is_equal))
                pick_first(one1)
                link("route", dve.scalar_tensor_tensor(out=lg[:, :, :], in0=one1[:, :, :], scalar=LOWEST, in1=lg[:, :, :],
                                                       op0=ALU.mult, op1=ALU.add))
                link("route", dve.tensor_reduce(top2[:, :], lg[:, :, :], AX.X, ALU.max))
                dve.tensor_tensor(gap[:, :], top2[:, :], top1[:, :], ALU.subtract).then_inc(Z["gap_ready"], 1)
                link("route", dve.tensor_tensor(eq[:, :, :], lg[:, :, :], bc_e(top2), ALU.is_equal))
                pick_first(one2)
                dve.tensor_tensor(both[:, :, :], one1[:, :, :], one2[:, :, :], ALU.add).then_inc(Z["both_ready"], 1)

            def route_gates():
                dve.wait_ge(Z["e2_ready"], 1)
                link("route", dve.tensor_scalar(den[:, :], e2[:, :], 1.0, None, ALU.add))
                link("route", dve.reciprocal(gate1[:, :], den[:, :]))
                link("route", dve.tensor_tensor(gate2[:, :], e2[:, :], gate1[:, :], ALU.mult))

            def route_slots():
                dve.wait_ge(Z["prefix_done"], 1)
                before = ps_o[:, BK // 4:BK // 4 + NT * NE].rearrange("p (j e) -> p j e", e=NE)
                totals = ps_o[:, BK // 2:BK // 2 + NT * NE].rearrange("p (j e) -> p e j", e=NE)
                link("route", dve.tensor_copy(tot[:, :, :], totals))
                flat = "p e j -> p (e j)"
                link("route", dve.tensor_tensor_scan(cum[:, :, :].rearrange(flat), first_tile[:, :, :].rearrange(flat),
                                                     tot[:, :, :].rearrange(flat), 0.0, ALU.mult, ALU.add))
                link("route", dve.tensor_tensor(eq[:, :, :].rearrange("p j e -> p (j e)").rearrange("p (e k) -> p e k", e=NE),
                                                cum[:, :, NT - 1:NT].to_broadcast([P, NE, NT]),
                                                thr[:, :].unsqueeze(1).to_broadcast([P, NE, NT]), ALU.is_gt))
                link("route", dve.tensor_reduce(tiles_e[:, :], eq[:, :, :].rearrange("p j e -> p (j e)").rearrange("p (e k) -> p e k", e=NE),
                                                AX.X, ALU.add))
                link("route", dve.tensor_tensor_scan(tiles_c[:, :], ones[:, 0:NE], tiles_e[:, :], 0.0, ALU.mult, ALU.add))
                link("route", dve.tensor_tensor(cmp[:, :, :], tile_no[:, :].unsqueeze(2).to_broadcast([P, MT, NE]),
                                                tiles_c[:, :].unsqueeze(1).to_broadcast([P, MT, NE]), ALU.is_ge))
                link("route", dve.tensor_reduce(texp_f[:, :], cmp[:, :, :], AX.X, ALU.add))
                dve.tensor_scalar(texp[:, :], texp_f[:, :], float(NE - 1), None, ALU.min).then_inc(Z["slots_ready"], 1)
                link("route", dve.tensor_tensor(tiles_x[:, :], tiles_c[:, :], tiles_e[:, :], ALU.subtract))
                link("route", dve.tensor_tensor(cum[:, :, :], cum[:, :, :], tot[:, :, :], ALU.subtract))
                link("route", dve.scalar_tensor_tensor(out=cum[:, :, :], in0=tiles_x[:, :].unsqueeze(2).to_broadcast([P, NE, NT]),
                                                       scalar=float(P), in1=cum[:, :, :], op0=ALU.mult, op1=ALU.add))
                link("route", dve.tensor_tensor(lg[:, :, :], before, cum[:, :, :].rearrange("p e j -> p j e"), ALU.add))
                link("route", dve.tensor_tensor(eq[:, :, :], lg[:, :, :], one1[:, :, :], ALU.mult))
                link("route", dve.tensor_reduce(pick[:, :], eq[:, :, :], AX.X, ALU.add))
                dve.tensor_copy(slot1[:, :], pick[:, :])
                link("route", dve.tensor_tensor(eq[:, :, :], lg[:, :, :], one2[:, :, :], ALU.mult))
                link("route", dve.tensor_reduce(top1[:, :], eq[:, :, :], AX.X, ALU.add))
                dve.tensor_copy(slot2[:, :], top1[:, :]).then_inc(Z["slots_ready"], 1)

            q_low(1)
            step(0, 0, tr=False)
            route_choice()
            step(0, 1)
            route_slots()
            step(0, 2)
            route_gates()
            q_low(2)
            step(0, 3)
            step(0, 4)
            step(0, 5)
            step(0, 6)

            def xgT_low(b):
                dve.wait_ge(Z["xgT_hi_ready"], b + 1)
                dve.tensor_tensor(xgT_lo[:, :], ps_m[:, :], raw(xgT_hi[:, :]), ALU.subtract).then_inc(Z["xgT_lo_ready"], 1)

            def l1_copy(b, u):
                i = b * TB + u
                dve.wait_ge(Z["l1_done"], i + 1)
                if not (exact(b) and i < 2):
                    dve.wait_ge(Z["midT_done"], i - 1)
                dve.tensor_copy(mid[:, u % 2, :], ps_s[:, u % 2, :]).then_inc(Z["l1_copied"], 1)

            def y_add(b, u, e):
                i = b * TB + u
                h = (u - 2) % TB // 2
                dve.wait_ge(Z["y_done"], i - 1)
                if u % 2 == 0 and not (exact(b) and i < 6):
                    dve.wait_ge(s_y[h], b * 16 if h == 0 else (b - 1) * 16)
                dve.tensor_tensor(y_sb[:, (u - 2) % TB, :], ps_s[:, 2 + u % 2, 0:D], b2_sb[:, bass.ds(e, 1), :].rearrange("p a d -> p (a d)"),
                                  ALU.add).then_inc(Z["y_ready"], 1)

            def moe_batch(b, last=False):
                start = 2 if exact(b) and b == 0 else 0
                experts = [None] * start + expert_of(dve, b * TB - 2 + start, TB - start)
                for u in range(TB):
                    l1_copy(b, u)
                    if u == TB - 1 and not last:
                        xgT_low(b + 1)
                    if u >= start:
                        y_add(b, u, experts[u])

            dve.wait_ge(Z["w1_split"], NE)
            xgT_low(0)
            moe_batch(0)
            moe_batch(1)
            with dve.Fori(2, MB - 1) as b:
                moe_batch(b)
            moe_batch(MB - 1, last=True)
            for u, e in enumerate(expert_of(dve, MT - 2, 2)):
                y_add(MB, u, e)

            def combine(j, zb, k):
                dve.wait_ge(s_z[zb], k * 32 + 32)
                dve.tensor_scalar(moe[:, bass.ds(j, 1), :].rearrange("p a d -> p (a d)"), z[:, zb, 0, :],
                                  gate1[:, bass.ds(j, 1)], None, ALU.mult).then_inc(Z["moe_link"], 1)
                dve.wait_ge(Z["moe_link"], j + 1)
                dve.scalar_tensor_tensor(out=moe[:, bass.ds(j, 1), :].rearrange("p a d -> p (a d)"), in0=z[:, zb, 1, :],
                                         scalar=gate2[:, bass.ds(j, 1)],
                                         in1=moe[:, bass.ds(j, 1), :].rearrange("p a d -> p (a d)"),
                                         op0=ALU.mult, op1=ALU.add).then_inc(Z["combined"], 1)

            with dve.Fori(1, NR - 1) as it:
                q_low(it + 2)
                for n in range(TB):
                    step(it, 3 + n)
                    for t in range(2):
                        combine(it * ZB + (2 * n + t - ZB), 2 * n + t, it - 1)
            step(NR - 1, 3)
            step(NR - 1, 4, scores=False)
            dve.wait_ge(Z["x_biased"], 2)

            def add_out(r):
                dve.wait_ge(Z["out_done"], r + 1)
                dve.tensor_tensor(x_sb[:, TB * r:TB * (r + 1), :], ps_s[:, r, :].rearrange("p (j e) -> p j e", e=D),
                                  x_sb[:, TB * r:TB * (r + 1), :], ALU.add).then_inc(Z["out_added"], 1)

            link("sums", dve.tensor_reduce(rinv[:, :], sums[:, :].rearrange("p (j b) -> p j b", b=NR), AX.X, ALU.add))
            link("sums", dve.reciprocal(rinv[:, :], rinv[:, :]))
            for r in range(NR):
                dve.wait_ge(Z["oTT_done"], r + 1)
                if r >= 2:
                    dve.wait_ge(Z["out_done"], r - 1)
                dve.tensor_tensor(o_sb[:, r % 2, :, :], ps_t[:, r % 2, :].rearrange("q (j d) -> q j d", d=D),
                                  rinv[:, TB * r:TB * (r + 1)].unsqueeze(2).to_broadcast([P, TB, D]),
                                  ALU.mult).then_inc(Z["o_ready"], 1)
                if r >= 1:
                    add_out(r - 1)
            add_out(NR - 1)

        @block.tensor
        def _(pe):
            def product(dst, lhs, rhs, start=True, stop=True):
                (lh, ll), (rh, rl) = lhs, rhs
                pe.matmul(dst, lh, rh, start=start, stop=False)
                pe.matmul(dst, lh, rl, start=False, stop=False)
                return pe.matmul(dst, ll, rh, start=False, stop=stop)

            def xnT(cols):
                return xnT_hi[:, cols], xnT_lo[:, cols]

            pe.wait_ge(Z["consts"], 9)
            pe.wait_ge(Z["w_loaded"], 16 * 7)
            pe.transpose(ps_m[:, 2 * D:3 * D], w_raw[:, 4, :], ident[:, :])
            pe.matmul(ps_m[:, 0:D], w_raw[:, 0, :], w_raw[:, 1, :], start=True, stop=True)
            pe.transpose(ps_m[:, 3 * D:3 * D + NE * HC], b1_rows, ident[0:NE * HC, 0:NE * HC])
            pe.transpose(ps_m[:, D:2 * D], w_raw[:, 2, :], ident[:, :]).then_inc(Z["wT_done"], 1)
            pe.transpose(ps_o[:, 0:D], w_raw[:, 3, :], ident[:, :])
            pe.wait_ge(Z["winT_ready"], 1)
            pe.matmul(ps_o[:, D:D + NE], winT, wg_sb[:, :], start=True, stop=True)
            pe.matmul(ps_o[:, D + NE:D + 2 * NE], bin_col[:, 0:1].to_broadcast([P, P]), wg_sb[:, :],
                      start=True, stop=True).then_inc(Z["gate_done"], 1)

            def xn_transpose(r):
                pe.wait_ge(Z["xn_ready"], 2 * (r + 1))
                pe.wait_ge(Z["xn_act_ready"], 2 * (r + 1))
                if r >= 2:
                    pe.wait_ge(Z["xT_lo"], r - 1)
                for j in range(TB):
                    last = pe.transpose(ps_t[:, r % 2, P * j:P * (j + 1)], xn[:, r % 2, j, :], ident[:, :])
                last.then_inc(Z["xT_done"], 1)

            for r in range(NR):
                xn_transpose(r)
            pe.wait_ge(Z["xT_lo"], NR)
            pe.wait_ge(Z["w_lo_ready"], 3)
            for j in range(NT):
                xh, xl = xnT(slice(P * j, P * (j + 1)))
                g = 2 * NE * j
                pe.matmul(ps_o[:, g:g + 2 * NE], xh, gate_w[:, :, :].rearrange("p t e -> p (t e)"), start=True, stop=False,
                          skip_group_check=True)
                last = pe.matmul(ps_o[:, g:g + NE], xl, gate_w[:, 0, :], start=False, stop=True, skip_group_check=True)
            last.then_inc(Z["logits_done"], 1)
            for n in range(NT // 2):
                if n >= NR:
                    pe.wait_ge(Z["v_lo_ready"], n - NR + 1)
                    pe.wait_ge(Z["rows_ready"], n - NR + 1)
                for j in range(2):
                    last = product(vt_bank(n)[:, j, :, :].rearrange("p t d -> p (t d)"), xnT(slice(P * (2 * n + j), P * (2 * n + j + 1))),
                                   [t[:, :, :].rearrange("p t d -> p (t d)") for t in (vt_hi, vt_lo)])
                last.then_inc(Z["vt_done"], 1)

            def q_project(it):
                product(ps_m[:, :], (mm_hi[:, :], mm_lo[:, :]), xnT(bass.ds(it * BK, BK))).then_inc(Z["q_done"], 1)

            def step(it, c, scores=True, tr=True, pv=True, q_next=None):
                i = it * TB + c
                if scores:
                    if c % TB == 0:
                        pe.wait_ge(Z["q_lo_ready"], it + (c // TB + 1))
                    for b in range(NR):
                        if not (exact(it) and i < 1):
                            pe.wait_ge(Z["exp_done"], (i - 1) * NR + (b + 1))
                        product(ps_s[:, b, :], (q_hi[:, P * (c % TB):P * (c % TB + 1)], q_lo[:, P * (c % TB):P * (c % TB + 1)]),
                                xnT(slice(BK * b, BK * (b + 1)))).then_inc(Z["scores_done"], 1)
                if q_next is not None:
                    q_project(q_next)
                g = it * 2 + ((c - 3) // 2)
                half = (c - 3) % 2
                for b in range(NR):
                    if tr:
                        if not scores:
                            pe.wait_ge(Z["exp_done"], (i - 1) * NR + (b + 1))
                        if not (exact(it) and i == 1 and b < 2):
                            pe.wait_ge(Z["pt_lo_ready"], (i - 1) * NR + (b - 1))
                        for k in range(TB):
                            at = BK * b + P * k
                            last = pe.transpose(ps_t[:, b % 2, P * k:P * (k + 1)], probs[:, at:at + P], ident[:, :])
                        last.then_inc(Z["pT_done"], 1)
                    if pv:
                        if b == 0 and half == 0:
                            pe.wait_ge(Z["pt_lo_ready"], (g + 1) * (2 * NR))
                            if not (exact(it) and it == 0 and c < 5):
                                pe.wait_ge(Z["oT_copied"], g)
                        G = (c - 3) // 2 % 2
                        for k in range(2):
                            ch = half * (NT // 2) + 2 * b + k
                            last = product(ps_o[:, 0:2 * P], (v_hi[:, ch, :], v_lo[:, ch, :]),
                                           (pt_hi[:, G, ch, :], pt_lo[:, G, ch, :]), start=(ch == 0), stop=(ch == NT - 1))
                        if ch == NT - 1:
                            last.then_inc(Z["pv_done"], 1)

            q_project(0)
            pe.wait_ge(Z["v_lo_ready"], NT // 2)
            pe.wait_ge(Z["rows_ready"], NT // 2)
            step(0, 0, tr=False, pv=False)
            step(0, 1, pv=False)
            pe.wait_ge(Z["both_ready"], 1)
            flat = both[:, :, :].rearrange("p j e -> p (j e)")
            pe.matmul(ps_o[:, BK // 4:BK // 4 + NT * NE], tri[:, :], flat, start=True, stop=True)
            pe.matmul(ps_o[:, BK // 2:BK // 2 + NT * NE], ones[:, :], flat, start=True, stop=True).then_inc(Z["prefix_done"], 1)
            step(0, 2, pv=False)
            pe.wait_ge(Z["slots_ready"], 2)
            step(0, 3, q_next=1)
            step(0, 4)
            step(0, 5)
            step(0, 6)

            def xg_transpose(b):
                pe.wait_ge(Z["xg_loaded"], (b + 1) * 16)
                if not (exact(b) and b == 0):
                    pe.wait_ge(Z["xgT_lo_ready"], b)
                for k in range(TB):
                    last = pe.transpose(ps_m[:, P * k:P * (k + 1)], xg[:, k, :], ident[:, :])
                last.then_inc(Z["xgT_done"], 1)

            def layer1(b, u, experts):
                e = experts[u]
                if u == 0:
                    pe.wait_ge(Z["xgT_lo_ready"], b + 1)
                at = slice(P * u, P * (u + 1))
                w1e = [t[:, bass.ds(e, 1), :].rearrange("p a h -> p (a h)") for t in (w1_hi, w1_lo)]
                product(ps_s[:, u % 2, :], (xgT_hi[:, at], xgT_lo[:, at]), w1e).then_inc(Z["l1_done"], 1)

            def mid_transpose(b, u):
                i = b * TB + u
                pe.wait_ge(Z["l1_copied"], i)
                for k in range(HC):
                    last = pe.transpose(ps_t[:, (u - 1) % 2, P * k:P * (k + 1)], mid[:, (u - 1) % 2, P * k:P * (k + 1)], ident[:, :])
                last.then_inc(Z["midT_done"], 1)

            def layer2(b, u, e):
                i = b * TB + u
                pe.wait_ge(Z["midT_ready"], (i - 1) * HC)
                if not (exact(b) and i < 4):
                    pe.wait_ge(Z["y_ready"], i - 3)
                for k in range(HC):
                    last = pe.matmul(ps_s[:, 2 + u % 2, 0:D], midT[:, u % 2, k, :],
                                     w2v[:, bass.ds(e, 1), k, :].rearrange("p a d -> p (a d)"),
                                     start=(k == 0), stop=(k == HC - 1))
                last.then_inc(Z["y_done"], 1)

            def moe_batch(b, last=False):
                now = expert_of(pe, b * TB, TB)
                before = [None] * 2 if exact(b) and b == 0 else expert_of(pe, b * TB - 2, 2)
                for u in range(TB):
                    layer1(b, u, now)
                    if u == TB - 1 and not last:
                        xg_transpose(b + 1)
                    if not (exact(b) and b == 0 and u < 1):
                        mid_transpose(b, u)
                    if not (exact(b) and b == 0 and u < 2):
                        layer2(b, u, (before + now)[u])

            pe.wait_ge(Z["exp_done"], 7 * NR)
            pe.wait_ge(Z["pt_lo_ready"], 6 * NR)
            pe.wait_ge(Z["w1_split"], NE)
            pe.wait_ge(Z["w2_loaded"], 32)
            xg_transpose(0)
            moe_batch(0)
            with pe.Fori(1, MB - 1) as b:
                moe_batch(b)
            moe_batch(MB - 1, last=True)
            mid_transpose(MB, 0)
            for u, e in enumerate(expert_of(pe, MT - 2, 2)):
                layer2(MB, u, e)
            pe.wait_ge(Z["l1_copied"], MT)
            pe.wait_ge(Z["y_ready"], MT)
            pe.wait_ge(Z["midT_ready"], MT * HC)

            with pe.Fori(1, NR - 1) as it:
                for n in range(TB):
                    step(it, 3 + n, q_next=it + 1 if n == 0 else None)
            step(NR - 1, 3)
            step(NR - 1, 4, scores=False)
            pe.wait_ge(Z["combined"], NT)
            for r in range(NR):
                pe.wait_ge(Z["exp_done"], NT * NR)
                for k in range(TB):
                    last = pe.transpose(ps_s[:, r, P * k:P * (k + 1)], moe[:, TB * r + k, :], ident[:, :])
                last.then_inc(Z["moeT_done"], 1)
            step(NR - 1, 5, scores=False, tr=False)
            step(NR - 1, 6, scores=False, tr=False)
            pe.wait_ge(Z["oT_copied"], NT // 2)
            pe.wait_ge(Z["moeT_ready"], NR)

            def o_transpose(r):
                if r >= 2:
                    pe.wait_ge(Z["o_ready"], r - 1)
                for k in range(TB):
                    last = pe.transpose(ps_t[:, r % 2, P * k:P * (k + 1)], oT_all[:, TB * r + k, :], ident[:, :])
                last.then_inc(Z["oTT_done"], 1)
            o_transpose(0)
            o_transpose(1)
            for r in range(NR):
                for k in range(TB):
                    dst = ps_s[:, r, P * k:P * (k + 1)]
                    pe.matmul(dst, moeT[:, P * (TB * r + k):P * (TB * r + k + 1)], wo_sb[:, :], start=True, stop=False)
                    if k == 0:
                        pe.wait_ge(Z["o_ready"], r + 1)
                    last = pe.matmul(dst, o_sb[:, r % 2, k, :], wpT[:, :], start=False, stop=True)
                last.then_inc(Z["out_done"], 1)
                if r + 2 < NR:
                    o_transpose(r + 2)


_INS = ['L0_attn_x', 'L0_attn_w_qkv', 'L0_attn_w_proj', 'L0_attn_b_proj', 'L0_ffn_W_in', 'L0_ffn_b_in',
        'L0_ffn_W_gate', 'L0_ffn_b_gate', 'L0_ffn_W1', 'L0_ffn_b1', 'L0_ffn_W2', 'L0_ffn_b2', 'L0_ffn_W_out',
        'L0_ffn_b_out']
_OUTS = [((1, 2048, 128), 'float32')]


def kernel(**inputs):
    import numpy as _np
    import concourse.bacc as _bacc
    from concourse import mybir as _mybir
    from concourse.bass_utils import run_bass_kernel_spmd as _run

    nc = _bacc.Bacc("TRN2", target_bir_lowering=False, num_devices=1)
    arrays, args = {}, []
    for name in _INS:
        a = _np.ascontiguousarray(inputs[name])
        arrays[f"in_{name}_dram"] = a
        args.append(nc.dram_tensor(f"in_{name}_dram", a.shape, _mybir.dt.from_np(a.dtype), kind="ExternalInput").ap())
    for i, (shape, dtype) in enumerate(_OUTS):
        dt = _mybir.dt.from_np(_np.dtype(dtype))
        args.append(nc.dram_tensor(f"out_{i}_dram", shape, dt, kind="ExternalOutput").ap())
    attention_moe_kernel(nc, *args)
    r = _run(nc, [arrays], core_ids=[0])
    return r.results[0]["out_0_dram"]
```

```python
import concourse.bass as bass
from concourse import mybir
from contextlib import ExitStack

FP32 = mybir.dt.float32
FP32R = mybir.dt.float32r
I32 = mybir.dt.int32
U32 = mybir.dt.uint32
ALU = mybir.AluOpType
ACT = mybir.ActivationFunctionType
AX = mybir.AxisListType


def attention_moe_kernel(nc, x, w_qkv, w_proj, b_proj, w_in, b_in, w_gate, b_gate,
                         w1, b1, w2, b2, w_out, b_out, out):
    P = 128
    S, D = x.shape[1], x.shape[2]
    NT = S // P
    NE, _, DM = w1.shape
    HC = DM // P
    BK = 512
    NR = S // BK
    TB = BK // P
    TOPK = 2
    VP = 5
    EP = 3
    MT = (TOPK * S + NE * (P - 1)) // P
    MB = -(-MT // TB)
    MS = MB * TB
    HEADS = 16
    SCALE = 1.0 / float(D // HEADS) ** 0.5
    EPS = 1e-5
    LOWEST = -3.0e38

    ctx = ExitStack()
    with ctx:
        def sb(name, shape, dt=FP32):
            return ctx.enter_context(nc.sbuf_tensor(name, shape, dt))

        def sem(name):
            return ctx.enter_context(nc.semaphore(name))

        slots_in = nc.dram_tensor("slots_in", (MS * P, D), FP32, kind="Internal").ap()
        slots_out = nc.dram_tensor("slots_out", (MT * P, D), FP32, kind="Internal").ap()

        x_sb = sb("x_sb", [P, NT, D])
        xnT_hi = sb("xnT_hi", [P, S], FP32R)
        xnT_lo = sb("xnT_lo", [P, S], FP32R)
        v_hi = sb("v_hi", [P, NT, D], FP32R)
        v_lo = sb("v_lo", [P, NT, D], FP32R)
        q_hi = sb("q_hi", [P, BK], FP32R)
        q_lo = sb("q_lo", [P, BK], FP32R)
        probs = sb("probs", [P, S])
        pt_hi = sb("pt_hi", [P, 2, NT, 2 * P], FP32R)
        pt_lo = sb("pt_lo", [P, 2, NT, 2 * P], FP32R)
        oT_all = sb("oT_all", [P, NT, P])
        w1_hi = sb("w1_hi", [P, NE, DM], FP32R)
        w1_lo = sb("w1_lo", [P, NE, DM], FP32R)
        w2_sb = sb("w2_sb", [P, NE * HC * D])
        w1_raw = sb("w1_raw", [P, 2, DM])
        mm_hi = sb("mm_hi", [P, D], FP32R)
        mm_lo = sb("mm_lo", [P, D], FP32R)
        vt_hi = sb("vt_hi", [P, 2, D], FP32R)
        vt_lo = sb("vt_lo", [P, 2, D], FP32R)
        gate_w = sb("gate_w", [P, 2, P], FP32R)
        wpT = sb("wpT", [P, D])
        wo_sb = sb("wo_sb", [P, D])
        ident = sb("ident", [P, P])
        tri = sb("tri", [P, P])
        ones = sb("ones", [P, P])
        bsum = sb("bsum", [P, 2, D])
        bin_col = sb("bin_col", [P, 1])
        wg_sb = sb("wg_sb", [P, NE])
        bg_sb = sb("bg_sb", [P, NE])
        b1_col = sb("b1_col", [P, NE, HC])
        b2_sb = sb("b2_sb", [P, NE, D])
        stats = sb("stats", [P, NT, 6])
        mv = sb("mv", [P, NT, 2])
        veps = sb("veps", [P, NT])
        std = sb("std", [P, NT])
        rstd = sb("rstd", [P, NT])
        newton = sb("newton", [P, NT])
        nmr = sb("nmr", [P, NT])
        gate_b = sb("gate_b", [P, NE])
        bank_max = sb("bank_max", [P, 2, NR])
        neg_max = sb("neg_max", [P, 2])
        sums = sb("sums", [P, NT * NR])
        rinv = sb("rinv", [P, NT])
        lg = sb("lg", [P, NT, NE])
        eq = sb("eq", [P, NT, NE])
        choice = sb("choice", [P, TOPK, NT, NE])
        slot_f = sb("slot_f", [P, TOPK, NT])
        both = sb("both", [P, NT, NE])
        desc = sb("desc", [P, NE])
        first_tile = sb("first_tile", [P, NE, NT])
        tot = sb("tot", [P, NE, NT])
        cum = sb("cum", [P, NE, NT])
        thr = sb("thr", [P, NT])
        tiles_e = sb("tiles_e", [P, NE])
        tiles_c = sb("tiles_c", [P, NE])
        tiles_x = sb("tiles_x", [P, NE])
        tile_no = sb("tile_no", [P, MS])
        cmp = sb("cmp", [P, MS, NE])
        texp_f = sb("texp_f", [P, MS])
        texp = sb("texp", [P, MS], I32)
        top1 = sb("top1", [P, NT])
        top2 = sb("top2", [P, NT])
        pick = sb("pick", [P, NT])
        gap = sb("gap", [P, NT])
        e2 = sb("e2", [P, NT])
        den = sb("den", [P, NT])
        gate1 = sb("gate1", [P, NT])
        gate2 = sb("gate2", [P, NT])
        slots = sb("slots", [P, TOPK, NT], I32)
        xgT_hi = sb("xgT_hi", [P, BK], FP32R)
        xgT_lo = sb("xgT_lo", [P, BK], FP32R)
        mid = sb("mid", [P, 2, DM])
        xn = probs[:, 0:2 * BK].rearrange("p (b j e) -> p b j e", b=2, e=D)
        xg = w1_raw[:, 0, :].rearrange("p (j d) -> p j d", d=D)
        y_sb = w1_raw[:, 1, :].rearrange("p (j d) -> p j d", d=D)
        w_raw = w2_sb[:, 0:5 * D].rearrange("p (t e) -> p t e", e=D)
        winT = w2_sb[:, 5 * D:6 * D]
        bin_rows = w2_sb[:, 6 * D:7 * D]
        t_rows = w2_sb[:, S:2 * S].rearrange("p (j d) -> p j d", d=D)
        w2v = w2_sb[:, :].rearrange("p (e c d) -> p e c d", e=NE, d=D)
        ZB = 8
        moe = w2_sb[:, 0:S].rearrange("p (j d) -> p j d", d=D)
        z = w2_sb[:, S:2 * S].rearrange("p (b t d) -> p b t d", b=ZB, d=D)
        o_sb = mid[:, :, :].rearrange("p b (j d) -> p b j d", d=D)
        moeT = w2_sb[:, S:2 * S]
        midT = oT_all[:, NT // 2:NT, :].rearrange("p (b c) n -> p b c n", b=2)
        b1_rows = mid[0:NE * HC, 0, 0:P]
        v_all = oT_all[:, :, :]

        def raw(ap):
            return ap.bitcast(FP32)

        ps_s = ctx.enter_context(nc.psum_tensor("ps_s", [P, NR, BK], FP32))
        ps_t = ctx.enter_context(nc.psum_tensor("ps_t", [P, 2, BK], FP32))
        ps_o = ctx.enter_context(nc.psum_tensor("ps_o", [P, BK], FP32))
        ps_m = ctx.enter_context(nc.psum_tensor("ps_m", [P, BK], FP32))

        Z = {n: sem(n) for n in """
            w_loaded b_loaded consts ones_ready zero_ready zeroed ln_link ln_std_in std_ready xn_ready
            xT_done xT_hi xT_lo wT_done w_hi_ready w_lo_ready winT_ready gate_done gate_ready x_biased
            vt_done v_hi_ready v_lo_ready rows_ready logits_done
            q_done q_hi_ready q_lo_ready scores_done part_max neg_max_ready exp_done
            pT_done pt_hi_ready pt_lo_ready pv_done oT_copied
            pick_link slots_link gates_link experts_link gap_ready e2_ready both_ready prefix_done
            slots_ready experts_ready scattered w1_late w1_split w2_loaded xn_act_ready ln_bias_ready w1_hi_ready
            xgT_done xgT_hi_ready xgT_lo_ready l1_done l1_copied midT_done midT_ready
            y_done y_ready combined moe_link moeT_done moeT_ready
            sums_link oTT_done o_ready out_done out_added stored
            """.split()}
        s_x = [sem(f"x_loaded{r}") for r in range(NR)]
        s_w1 = [sem(f"w1_loaded{r}") for r in range(2)]
        s_xg = [sem(f"xg_loaded{r}") for r in range(2)]
        s_y = [sem(f"y_stored{r}") for r in range(2)]
        s_z = [sem(f"z_loaded{r}") for r in range(ZB)]

        def expert_of(eng, first, n):
            _, values = nc.values_load_multi_w_load_instructions(
                texp[0:1, bass.ds(first, n)], engines=[eng.engine], min_val=0, max_val=NE - 1,
                skip_runtime_bounds_check_because="a count of experts that is clamped to the last one")
            return list(values)

        def exact(it):
            return isinstance(it, int)

        def vt_bank(n):
            return ps_t[:, n % 2, :].rearrange("p (j t d) -> p j t d", j=2, t=2)

        PG = P // NR

        def q_view(t):
            return t[:, :].rearrange("e (p j) -> e j p", j=NT)

        q_psum = ps_m[:, :].rearrange("e (j p) -> e j p", j=NT)

        block = ctx.enter_context(nc.Block())

        @block.sync
        def _(sp):
            xv = x.rearrange("o (p j) e -> p (o j) e", p=P)
            for r in range(NR):
                sp.dma_start(x_sb[:, TB * r:TB * (r + 1), :], xv[:, TB * r:TB * (r + 1), :]).then_inc(s_x[r], 16)
            sp.wait_ge(Z["w_loaded"], 16 * 7)
            zero = pt_hi[:, 1, :, :].rearrange("p a b -> p (a b)").bitcast(FP32)
            zv = slots_in.rearrange("(b p r) d -> b p (r d)", p=P, b=2)
            for e in range(NE):
                if 2 <= e < EP + 2:
                    sp.wait_ge(Z["w1_split"], e - 1)
                elif e >= EP + 2:
                    sp.wait_ge(Z["w1_late"], e - (EP + 1))
                sp.dma_start(w1_raw[:, e % 2, :], w1[e]).then_inc(s_w1[e % 2], 16)
                if e == 1:
                    sp.wait_ge(Z["zero_ready"], 1)
                    for h in range(2):
                        sp.dma_start(zv[h], zero[:, 0:MS // 2 * D]).then_inc(Z["zeroed"], 16)
            w2_src = w2.rearrange("e (c p) d -> p e c d", p=P)
            sp.wait_ge(Z["w_lo_ready"], 2)
            sp.wait_ge(Z["gate_done"], 1)
            sp.dma_start(w2v[:, 0:NE // 2], w2_src[:, 0:NE // 2]).then_inc(Z["w2_loaded"], 16)

            xg_src = slots_in.rearrange("(t p) d -> p t d", p=P)
            y_dst = slots_out.rearrange("(t p) d -> p t d", p=P)

            def load_xg(b, g):
                sp.dma_start(xg[:, 2 * g:2 * g + 2, :], xg_src[:, bass.ds(b * TB + 2 * g, 2), :]).then_inc(s_xg[g], 16)

            def store_y(b, h):
                sp.wait_ge(Z["y_ready"], b * TB + (2 * h + 2))
                sp.dma_start(y_dst[:, bass.ds(b * TB + 2 * h, 2), :], y_sb[:, 2 * h:2 * h + 2, :]).then_inc(s_y[h], 16)

            sp.wait_ge(Z["scattered"], 16 * TOPK * NT)
            sp.wait_ge(Z["w1_late"], NE - EP)
            load_xg(0, 0)
            load_xg(0, 1)
            sp.dma_start(w2v[:, NE // 2:NE], w2_src[:, NE // 2:NE]).then_inc(Z["w2_loaded"], 16)

            def next_xg(b):
                for g in range(2):
                    sp.wait_ge(Z["xgT_done"], b * 2 + (g + 1))
                    load_xg(b + 1, g)

            next_xg(0)
            store_y(0, 0)
            with sp.Fori(1, MB - 1) as b:
                next_xg(b)
                store_y(b - 1, 1)
                store_y(b, 0)
            store_y(MB - 2, 1)
            store_y(MB - 1, 0)
            sp.wait_ge(Z["y_ready"], MT)
            sp.dma_start(y_dst[:, MT - 1:MT, :], y_sb[:, 2:3, :]).then_inc(s_y[1], 16)
            ov = out.rearrange("o (p j) e -> p (o j) e", p=P)
            for r in range(NR):
                sp.wait_ge(Z["out_added"], r + 1)
                sp.dma_start(ov[:, TB * r:TB * (r + 1), :], x_sb[:, TB * r:TB * (r + 1), :]).then_inc(Z["stored"], 16)
            sp.wait_ge(Z["stored"], 16 * NR)

        @block.gpsimd
        def _(pool):
            pool.memset(ident[:, :], 0.0).then_inc(Z["consts"], 1)
            pool.memset(first_tile[:, :, :], 1.0).then_inc(Z["consts"], 1)
            pool.memset(raw(gate_w[:, :, :]), 0.0).then_inc(Z["consts"], 1)
            pool.iota(desc[:, :], pattern=[[-1, NE]], base=NE, channel_multiplier=0,
                      allow_small_or_imprecise_dtypes=True).then_inc(Z["consts"], 1)
            pool.iota(thr[:, :], pattern=[[P, NT]], base=0, channel_multiplier=0,
                      allow_small_or_imprecise_dtypes=True).then_inc(Z["consts"], 1)
            pool.iota(tile_no[:, :], pattern=[[1, MS]], base=0, channel_multiplier=0,
                      allow_small_or_imprecise_dtypes=True).then_inc(Z["consts"], 1)
            pool.wait_ge(Z["consts"], 6)
            pool.wait_ge(Z["ones_ready"], 1)
            pool.affine_select(out=ident[:, :], in_=ident[:, :], compare_op=ALU.not_equal, fill=1.0,
                               base=0, pattern=[[-1, P]], channel_multiplier=1).then_inc(Z["consts"], 1)
            pool.affine_select(out=tri[:, :], in_=ones[:, :], compare_op=ALU.is_gt, fill=0.0,
                               base=0, pattern=[[1, P]], channel_multiplier=-1).then_inc(Z["consts"], 1)
            pool.affine_select(out=first_tile[:, :, :], in_=first_tile[:, :, :], compare_op=ALU.is_gt, fill=0.0,
                               base=0, pattern=[[0, NE], [1, NT]], channel_multiplier=0).then_inc(Z["consts"], 1)
            pool.memset(raw(pt_hi[:, 1, :, :]), 0.0).then_inc(Z["zero_ready"], 1)

            def w1_split(e):
                pool.wait_ge(s_w1[e % 2], 16 * (e // 2 + 1))
                pool.tensor_copy(w1_hi[:, e, :], w1_raw[:, e % 2, :]).then_inc(Z["w1_hi_ready"], 1)
                pool.wait_ge(Z["w1_hi_ready"], e + 1)
                pool.tensor_tensor(w1_lo[:, e, :], w1_raw[:, e % 2, :], raw(w1_hi[:, e, :]),
                                   ALU.subtract).then_inc(Z["w1_split"], 1)

            def v_low(n):
                pool.wait_ge(Z["v_hi_ready"], 2 * n + 2)
                pool.tensor_tensor(v_lo[:, 2 * n:2 * n + 2, :], v_all[:, 2 * n:2 * n + 2, :], raw(v_hi[:, 2 * n:2 * n + 2, :]),
                                   ALU.subtract).then_inc(Z["v_lo_ready"], 1)

            w1_split(0)
            w1_split(1)
            v_low(0)
            v_low(1)
            w1_split(2)
            for n in range(2, VP):
                v_low(n)
            pool.wait_ge(Z["zeroed"], 32)
            pool.wait_ge(Z["slots_ready"], 1)
            for j in range(NT):
                if j % 2 == 0:
                    pool.wait_ge(Z["rows_ready"], j // 2 + 1)
                for c in range(TOPK):
                    pool.indirect_dma_start(out=slots_in, out_offset=bass.IndirectOffsetOnAxis(ap=slots[:, c, j:j + 1], axis=0),
                                            in_=t_rows[:, j, :], in_offset=None).then_inc(Z["scattered"], 16)
            pool.wait_ge(Z["b_loaded"], 16 * 4)
            pool.wait_ge(Z["xn_ready"], NT // 2)
            pool.wait_ge(Z["xn_act_ready"], NT // 2)
            pool.tensor_tensor(bsum[:, 0, :], bsum[:, 0, :], bsum[:, 1, :], ALU.add).then_inc(Z["x_biased"], 1)
            pool.wait_ge(Z["x_biased"], 1)
            pool.tensor_tensor(x_sb[:, :, :], x_sb[:, :, :], bsum[:, 0:1, :].to_broadcast([P, NT, D]),
                               ALU.add).then_inc(Z["x_biased"], 1)
            for h in range(2):
                pool.wait_ge(s_y[h], 16 * MB)
            pool.wait_ge(Z["y_done"], MT)
            for j in range(NT):
                if j >= ZB:
                    pool.wait_ge(Z["combined"], j - ZB + 1)
                for c in range(TOPK):
                    pool.indirect_dma_start(out=z[:, j % ZB, c, :], out_offset=None, in_=slots_out,
                                            in_offset=bass.IndirectOffsetOnAxis(ap=slots[:, c, j:j + 1], axis=0)
                                            ).then_inc(s_z[j % ZB], 16)

        @block.scalar
        def _(act):
            act.preload_act_table(ACT.Sqrt)
            wv_ = w_qkv.rearrange("(t p) e -> p t e", p=P)
            act.dma_start(w_raw[:, 0:3, :], wv_).then_inc(Z["w_loaded"], 16)
            act.dma_start(w_raw[:, 3, :], w_proj).then_inc(Z["w_loaded"], 16)
            act.dma_start(w_raw[:, 4, :], w_in).then_inc(Z["w_loaded"], 16)
            act.dma_start(wo_sb[:, :], w_out).then_inc(Z["w_loaded"], 16)
            act.dma_start(wg_sb[:, :], w_gate).then_inc(Z["w_loaded"], 16)
            act.dma_start(bin_col[:, :], b_in.rearrange("(p a) -> p a", a=1)).then_inc(Z["w_loaded"], 16)
            act.dma_start(b1_rows, b1.rearrange("e (c p) -> (e c) p", p=P)).then_inc(Z["w_loaded"], 16)

            def rows(v, n):
                return v.rearrange("(a n) -> a n", a=1).to_broadcast([P, n])
            act.dma_start(bsum[:, 0, :], rows(b_proj, D)).then_inc(Z["b_loaded"], 16)
            act.dma_start(bsum[:, 1, :], rows(b_out, D)).then_inc(Z["b_loaded"], 16)
            act.dma_start(bg_sb[:, :], rows(b_gate, NE)).then_inc(Z["b_loaded"], 16)
            act.dma_start(b2_sb[:, :, :].rearrange("p e d -> p (e d)"),
                          b2.rearrange("(a e) d -> a (e d)", a=1).to_broadcast([P, NE * D])).then_inc(Z["b_loaded"], 16)

            def ln_sqrt(h):
                at = slice(NT // 2 * h, NT // 2 * (h + 1))
                act.wait_ge(Z["ln_std_in"], h + 1)
                act.activation(std[:, at], veps[:, at], ACT.Sqrt).then_inc(Z["std_ready"], 1)

            ln_sqrt(0)
            act.wait_ge(Z["wT_done"], 1)
            act.activation(winT, ps_m[:, 2 * D:3 * D], ACT.Copy).then_inc(Z["winT_ready"], 1)
            act.activation(vt_hi[:, 0, :], ps_m[:, D:2 * D], ACT.Copy).then_inc(Z["w_hi_ready"], 1)
            act.activation(vt_hi[:, 1, :], w_raw[:, 4, :], ACT.Copy).then_inc(Z["w_hi_ready"], 1)
            act.activation(mm_hi[:, :], ps_m[:, 0:D], ACT.Copy).then_inc(Z["w_hi_ready"], 1)
            act.activation(b1_col[:, :, :].rearrange("p e c -> p (e c)"), ps_m[:, 3 * D:3 * D + NE * HC],
                           ACT.Copy).then_inc(Z["w_hi_ready"], 1)

            def normalise(r):
                if r >= 2:
                    act.wait_ge(Z["xT_done"], r - 1)
                for j in range(TB * r + 2, TB * (r + 1)):
                    act.activation(xn[:, r % 2, j % TB, :], x_sb[:, j, :], ACT.Identity, bias=nmr[:, j:j + 1],
                                   scale=rstd[:, j:j + 1]).then_inc(Z["xn_act_ready"], 1)

            def xT_high(r):
                act.wait_ge(Z["xT_done"], r + 1)
                act.activation(xnT_hi[:, BK * r:BK * (r + 1)], ps_s[:, r, :], ACT.Copy).then_inc(Z["xT_hi"], 1)

            def vt_high(n):
                act.wait_ge(Z["vt_done"], n + 1)
                act.activation(v_all[:, 2 * n:2 * n + 2, :], vt_bank(n)[:, :, 0, :], ACT.Copy).then_inc(Z["v_hi_ready"], 1)
                act.activation(v_hi[:, 2 * n:2 * n + 2, :], vt_bank(n)[:, :, 0, :], ACT.Copy).then_inc(Z["v_hi_ready"], 1)
                act.activation(t_rows[:, 2 * n:2 * n + 2, :], vt_bank(n)[:, :, 1, :], ACT.Copy).then_inc(Z["rows_ready"], 1)

            def q_split(n):
                act.wait_ge(Z["q_done"], n)
                act.activation(q_view(q_hi), q_psum, ACT.Copy, scale=SCALE).then_inc(Z["q_hi_ready"], 1)

            act.wait_ge(Z["ln_bias_ready"], 1)
            normalise(0)
            normalise(1)
            ln_sqrt(1)
            for r in range(NR):
                xT_high(r)
                if r == 0:
                    act.wait_ge(Z["gate_done"], 1)
                    act.wait_ge(Z["consts"], 9)
                    act.activation(gate_w[:, :, 0:NE], ps_o[:, D:D + NE].unsqueeze(1).to_broadcast([P, 2, NE]),
                                   ACT.Copy).then_inc(Z["gate_ready"], 1)
                    act.activation(wpT[:, :], ps_o[:, 0:D], ACT.Copy).then_inc(Z["gate_ready"], 1)
                    act.wait_ge(Z["ln_bias_ready"], 2)
                if r + 2 < NR:
                    normalise(r + 2)
                if r == 1:
                    act.preload_act_table(ACT.Exp)
                if r >= 2:
                    vt_high(r - 2)
            q_split(1)

            def xgT_high(b, g):
                act.wait_ge(Z["xgT_done"], b * 2 + (g + 1))
                act.activation(xgT_hi[:, 2 * P * g:2 * P * (g + 1)], ps_m[:, 2 * P * g:2 * P * (g + 1)], ACT.Identity,
                               bias=bin_col[:, 0:1]).then_inc(Z["xgT_hi_ready"], 1)

            def step(it, c, scores=True, tr=True, between=(None,) * NR):
                i = it * TB + c

                def hi_half(b):
                    if b == 0 and (c - 1) % 2 == 0 and not (exact(it) and i < 5):
                        act.wait_ge(Z["pv_done"], it * 2 + ((c - 1) // 2 - 1))
                    act.wait_ge(Z["pT_done"], (i - 1) * NR + (b + 1))
                    act.activation(pt_hi[:, (c - 1) // 2 % 2, TB * b:TB * (b + 1), P * ((c - 1) % 2):P * ((c - 1) % 2 + 1)],
                                   ps_t[:, b % 2, :].rearrange("k (c q) -> k c q", q=P),
                                   ACT.Copy).then_inc(Z["pt_hi_ready"], 1)

                def exp(b):
                    if b == 0:
                        act.wait_ge(Z["neg_max_ready"], i + 1)
                    act.activation(probs[:, BK * b:BK * (b + 1)], ps_s[:, b, :], ACT.Exp,
                                   bias=neg_max[:, c % 2:c % 2 + 1],
                                   accum_out=sums[:, bass.ds(i * NR + b, 1)]).then_inc(Z["exp_done"], 1)

                if tr:
                    hi_half(0)
                for b in range(NR):
                    if tr and b + 1 < NR:
                        hi_half(b + 1)
                    if scores:
                        exp(b)
                    if between[b]:
                        between[b]()

            def copy_o(g):
                act.wait_ge(Z["pv_done"], g + 1)
                act.activation(oT_all[:, bass.ds(g * 2, 2), :], ps_o[:, 0:2 * P].rearrange("p (a b) -> p a b", a=2),
                               ACT.Copy).then_inc(Z["oT_copied"], 1)

            def w1_high(e):
                act.wait_ge(s_w1[e % 2], 16 * (e // 2 + 1))
                act.activation(w1_hi[:, e, :], w1_raw[:, e % 2, :], ACT.Copy).then_inc(Z["w1_hi_ready"], 1)

            def vt_highs(*ns):
                for n in ns:
                    vt_high(n)

            vt_highs(2, 3)
            step(0, 0, tr=False, between=(None, lambda: vt_high(4), None, None))
            vt_highs(5, 6, 7)
            act.wait_ge(Z["w1_hi_ready"], EP)
            w1_high(3)
            step(0, 1)
            w1_high(4)
            step(0, 2)
            q_split(2)
            act.wait_ge(Z["v_lo_ready"], NT // 2)
            act.wait_ge(Z["zeroed"], 32)
            w1_high(5)
            act.wait_ge(Z["gap_ready"], 1)
            act.activation(e2[:, :], gap[:, :], ACT.Exp).then_inc(Z["e2_ready"], 1)
            step(0, 3)
            w1_high(6)
            step(0, 4)
            copy_o(0)
            w1_high(7)
            step(0, 5)
            step(0, 6, between=(lambda: xgT_high(0, 0), None, None, None))
            copy_o(1)

            def moe_relu(b, u, e):
                i = b * TB + u
                act.wait_ge(Z["midT_done"], i)
                if not (exact(b) and i < 3):
                    act.wait_ge(Z["y_done"], i - 2)
                for c in range(HC):
                    act.activation(midT[:, (u - 1) % 2, c, :], ps_t[:, (u - 1) % 2, P * c:P * (c + 1)], ACT.Relu,
                                   bias=b1_col[:, bass.ds(e, 1), c]).then_inc(Z["midT_ready"], 1)

            act.wait_ge(Z["experts_ready"], 1)

            def moe_batch(b, last=False, start=0):
                experts = [None] * start + expert_of(act, b * TB - 1 + start, TB - start)
                for u in range(TB):
                    if u >= start:
                        moe_relu(b, u, experts[u])
                    if u == 0:
                        xgT_high(b, 1)
                    if u == 2 and not last:
                        xgT_high(b + 1, 0)
            moe_batch(0, start=1)
            with act.Fori(1, MB - 1) as b:
                moe_batch(b)
            moe_batch(MB - 1, last=True)

            def attention_group(it):
                q_split(it + 2)
                step(it, 3)
                step(it, 4)
                copy_o(it * 2)
                step(it, 5)
                step(it, 6)
                copy_o(it * 2 + 1)

            with act.Fori(1, NR - 1) as it:
                attention_group(it)
            step(NR - 1, 3)
            step(NR - 1, 4, scores=False)
            copy_o(NT // 2 - 2)
            for r in range(NR):
                act.wait_ge(Z["moeT_done"], r + 1)
                act.activation(moeT[:, BK * r:BK * (r + 1)], ps_s[:, r, :], ACT.Copy).then_inc(Z["moeT_ready"], 1)
            copy_o(NT // 2 - 1)

        @block.vector
        def _(dve):
            count = {"ln": 0, "pick": 0, "slots": 0, "experts": 0, "gates": 0, "sums": 0}

            def link(key, inst):
                count[key] += 1
                s = Z[key + "_link"]
                inst.then_inc(s, 1)
                dve.wait_ge(s, count[key])

            dve.memset(ones[:, :], 1.0).then_inc(Z["ones_ready"], 1)

            def ln_stats(r):
                dve.wait_ge(s_x[r], 16)
                for j in range(TB * r, TB * (r + 1)):
                    dve.bn_stats(stats[:, j, :], x_sb[:, j, :]).then_inc(Z["ln_link"], 1)
                    count["ln"] += 1

            def ln_aggregate(h):
                dve.wait_ge(Z["ln_link"], count["ln"])
                for j in range(NT // 2 * h, NT // 2 * (h + 1)):
                    last = dve.bn_aggr(mv[:, j, :], stats[:, j, :])
                at = slice(NT // 2 * h, NT // 2 * (h + 1))
                link("ln", last)
                link("ln", dve.tensor_scalar(veps[:, at], mv[:, at, 1], EPS, None, ALU.add))
                dve.tensor_scalar(newton[:, at], veps[:, at], -0.5, None, ALU.mult).then_inc(Z["ln_std_in"], 1)

            def ln_scale(h):
                at = slice(NT // 2 * h, NT // 2 * (h + 1))
                dve.wait_ge(Z["std_ready"], h + 1)
                link("ln", dve.reciprocal(rstd[:, at], std[:, at]))
                link("ln", dve.tensor_tensor(nmr[:, at], rstd[:, at], rstd[:, at], ALU.mult))
                link("ln", dve.tensor_tensor(newton[:, at], newton[:, at], nmr[:, at], ALU.mult))
                link("ln", dve.scalar_tensor_tensor(out=rstd[:, at], in0=newton[:, at], scalar=1.5, in1=rstd[:, at],
                                                    op0=ALU.add, op1=ALU.mult))
                dve.scalar_tensor_tensor(out=nmr[:, at], in0=mv[:, at, 0], scalar=-1.0, in1=rstd[:, at],
                                         op0=ALU.mult, op1=ALU.mult).then_inc(Z["ln_bias_ready"], 1)

            def normalise(r):
                if r >= 2:
                    dve.wait_ge(Z["xT_done"], r - 1)
                for j in range(TB * r, TB * r + 2):
                    dve.tensor_scalar(xn[:, r % 2, j % TB, :], x_sb[:, j, :], mv[:, j, 0:1], rstd[:, j:j + 1],
                                      ALU.subtract, ALU.mult).then_inc(Z["xn_ready"], 1)

            def xT_low(r):
                at = slice(BK * r, BK * (r + 1))
                dve.wait_ge(Z["xT_hi"], r + 1)
                dve.tensor_tensor(xnT_lo[:, at], ps_s[:, r, :], raw(xnT_hi[:, at]), ALU.subtract).then_inc(Z["xT_lo"], 1)

            def q_low(n):
                dve.wait_ge(Z["q_hi_ready"], n)
                dve.scalar_tensor_tensor(out=q_view(q_lo), in0=q_psum, scalar=SCALE, in1=raw(q_view(q_hi)),
                                         op0=ALU.mult, op1=ALU.subtract).then_inc(Z["q_lo_ready"], 1)

            ln_stats(0)
            ln_stats(1)
            ln_aggregate(0)
            ln_stats(2)
            ln_scale(0)
            normalise(0)
            ln_stats(3)
            ln_aggregate(1)
            normalise(1)
            ln_scale(1)
            dve.wait_ge(Z["w_hi_ready"], 4)
            dve.tensor_tensor(vt_lo[:, 0, :], ps_m[:, D:2 * D], raw(vt_hi[:, 0, :]), ALU.subtract)
            dve.tensor_tensor(vt_lo[:, 1, :], w_raw[:, 4, :], raw(vt_hi[:, 1, :]), ALU.subtract).then_inc(Z["w_lo_ready"], 1)
            dve.tensor_tensor(mm_lo[:, :], ps_m[:, 0:D], raw(mm_hi[:, :]), ALU.subtract).then_inc(Z["w_lo_ready"], 1)
            for r in range(NR):
                xT_low(r)
                if r == 0:
                    dve.wait_ge(Z["gate_ready"], 2)
                    dve.wait_ge(Z["b_loaded"], 16 * 4)
                    dve.tensor_tensor(gate_w[:, 0, NE:2 * NE], ps_o[:, D:D + NE], raw(gate_w[:, 0, 0:NE]), ALU.subtract)
                    dve.tensor_tensor(gate_b[:, :], ps_o[:, D + NE:D + 2 * NE], bg_sb[:, :], ALU.add).then_inc(Z["w_lo_ready"], 1)
                if r + 2 < NR:
                    normalise(r + 2)

            def xgT_low(b, g):
                dve.wait_ge(Z["xgT_hi_ready"], b * 2 + (g + 1))
                at = slice(2 * P * g, 2 * P * (g + 1))
                dve.scalar_tensor_tensor(out=xgT_lo[:, at], in0=ps_m[:, at], scalar=bin_col[:, 0:1], in1=raw(xgT_hi[:, at]),
                                         op0=ALU.add, op1=ALU.subtract).then_inc(Z["xgT_lo_ready"], 1)

            def step(it, c, scores=True, tr=True, early=(None,) * NR, then=None, between=(None,) * NR):
                i = it * TB + c
                if scores:
                    for b in range(NR):
                        dve.wait_ge(Z["scores_done"], i * NR + (b + 1))
                        dve.tensor_reduce(bank_max[:, c % 2, b:b + 1], ps_s[:, b, :], AX.X, ALU.max).then_inc(Z["part_max"], 1)
                        if early[b]:
                            early[b]()
                    dve.wait_ge(Z["part_max"], (i + 1) * NR)
                    dve.tensor_reduce(neg_max[:, c % 2:c % 2 + 1], bank_max[:, c % 2, :], AX.X, ALU.max,
                                      negate=True).then_inc(Z["neg_max_ready"], 1)
                if then is not None:
                    then()
                for b in range(NR):
                    if tr:
                        G = (c - 1) // 2 % 2
                        at = (slice(None), G, slice(TB * b, TB * (b + 1)), slice(P * ((c - 1) % 2), P * ((c - 1) % 2 + 1)))
                        dve.wait_ge(Z["pt_hi_ready"], (i - 1) * NR + (b + 1))
                        dve.tensor_tensor(pt_lo[at], ps_t[:, b % 2, :].rearrange("k (c q) -> k c q", q=P),
                                          raw(pt_hi[at]), ALU.subtract).then_inc(Z["pt_lo_ready"], 1)
                    if between[b]:
                        between[b]()

            every = (slice(None),) * 3

            def bc_e(t):
                return t[:, :].unsqueeze(2).to_broadcast([P, NT, NE])

            def pick_first(c):
                link("pick", dve.tensor_tensor(eq[every], eq[every], desc[:, :].unsqueeze(1).to_broadcast([P, NT, NE]), ALU.mult))
                link("pick", dve.tensor_reduce(pick[:, :], eq[every], AX.X, ALU.max))
                return dve.tensor_tensor(choice[:, c, :, :], eq[every], bc_e(pick), ALU.is_equal)

            def route_logits():
                dve.wait_ge(Z["logits_done"], 1)
                parts = ps_o[:, 0:2 * NT * NE].rearrange("p (j t e) -> p j t e", t=2, e=NE)
                link("pick", dve.tensor_tensor(lg[every], parts[:, :, 1, :], gate_b[:, :].unsqueeze(1).to_broadcast([P, NT, NE]), ALU.add))
                link("pick", dve.tensor_tensor(lg[every], parts[:, :, 0, :], lg[every], ALU.add))

            def route_first():
                link("pick", dve.tensor_reduce(top1[:, :], lg[every], AX.X, ALU.max))
                link("pick", dve.tensor_tensor(eq[every], lg[every], bc_e(top1), ALU.is_equal))
                link("pick", pick_first(0))

            def route_second():
                link("pick", dve.scalar_tensor_tensor(out=lg[every], in0=choice[:, 0, :, :], scalar=LOWEST, in1=lg[every],
                                                      op0=ALU.mult, op1=ALU.add))
                link("pick", dve.tensor_reduce(top2[:, :], lg[every], AX.X, ALU.max))
                link("pick", dve.tensor_tensor(eq[every], lg[every], bc_e(top2), ALU.is_equal))
                dve.tensor_tensor(gap[:, :], top2[:, :], top1[:, :], ALU.subtract).then_inc(Z["gap_ready"], 1)
                link("pick", pick_first(1))
                dve.tensor_tensor(both[every], choice[:, 0, :, :], choice[:, 1, :, :], ALU.add).then_inc(Z["both_ready"], 1)

            def route_slots():
                dve.wait_ge(Z["prefix_done"], 1)
                below, total = [ps_o[:, BK // 4 * k:BK // 4 * (k + 1)].rearrange("p (j e) -> p j e", e=NE) for k in (1, 2)]
                flat = "p e j -> p (e j)"
                link("slots", dve.tensor_copy(tot[every], total.rearrange("p j e -> p e j")))
                link("slots", dve.tensor_tensor_scan(cum[every].rearrange(flat), first_tile[every].rearrange(flat),
                                                     tot[every].rearrange(flat), 0.0, ALU.mult, ALU.add))
                over = eq[every].rearrange("p j e -> p (j e)").rearrange("p (e k) -> p e k", e=NE)
                link("slots", dve.tensor_tensor(over, cum[:, :, NT - 1:NT].to_broadcast([P, NE, NT]),
                                                thr[:, :].unsqueeze(1).to_broadcast([P, NE, NT]), ALU.is_gt))
                dve.tensor_tensor(cum[every], cum[every], tot[every], ALU.subtract)
                link("slots", dve.tensor_reduce(tiles_e[:, :], over, AX.X, ALU.add))
                link("slots", dve.tensor_tensor_scan(tiles_c[:, :], ones[:, 0:NE], tiles_e[:, :], 0.0, ALU.mult, ALU.add))
                link("slots", dve.tensor_tensor(tiles_x[:, :], tiles_c[:, :], tiles_e[:, :], ALU.subtract))
                link("slots", dve.scalar_tensor_tensor(out=cum[every], in0=tiles_x[:, :].unsqueeze(2).to_broadcast([P, NE, NT]),
                                                       scalar=float(P), in1=cum[every], op0=ALU.mult, op1=ALU.add))
                link("slots", dve.tensor_tensor(lg[every], below, cum[every].rearrange("p e j -> p j e"), ALU.add))
                link("slots", dve.tensor_tensor(choice[:, :, :, :], choice[:, :, :, :],
                                                lg[every].unsqueeze(1).to_broadcast([P, TOPK, NT, NE]), ALU.mult))
                link("slots", dve.tensor_reduce(slot_f[:, :, :], choice[:, :, :, :], AX.X, ALU.add))
                dve.tensor_copy(slots[:, :, :], slot_f[:, :, :]).then_inc(Z["slots_ready"], 1)

            def route_experts():
                link("experts", dve.tensor_tensor(cmp[every], tile_no[:, :].unsqueeze(2).to_broadcast([P, MS, NE]),
                                                  tiles_c[:, :].unsqueeze(1).to_broadcast([P, MS, NE]), ALU.is_ge))
                link("experts", dve.tensor_reduce(texp_f[:, :], cmp[every], AX.X, ALU.add))
                dve.tensor_scalar(texp[:, :], texp_f[:, :], float(NE - 1), None, ALU.min).then_inc(Z["experts_ready"], 1)

            def route_gates():
                dve.wait_ge(Z["e2_ready"], 1)
                link("gates", dve.tensor_scalar(den[:, :], e2[:, :], 1.0, None, ALU.add))
                link("gates", dve.reciprocal(gate1[:, :], den[:, :]))
                dve.tensor_tensor(gate2[:, :], e2[:, :], gate1[:, :], ALU.mult)

            def w1_low(e):
                dve.wait_ge(Z["w1_hi_ready"], e + 1)
                dve.tensor_tensor(w1_lo[:, e, :], w1_raw[:, e % 2, :], raw(w1_hi[:, e, :]), ALU.subtract).then_inc(Z["w1_late"], 1)

            def v_lows():
                for n in range(VP, NT // 2):
                    dve.wait_ge(Z["v_hi_ready"], 2 * n + 2)
                    dve.tensor_tensor(v_lo[:, 2 * n:2 * n + 2, :], v_all[:, 2 * n:2 * n + 2, :],
                                      raw(v_hi[:, 2 * n:2 * n + 2, :]), ALU.subtract).then_inc(Z["v_lo_ready"], 1)

            route_logits()
            route_first()
            q_low(1)
            route_second()
            step(0, 0, tr=False, between=(route_slots, None, None, None))
            step(0, 1, then=v_lows, between=(None, lambda: w1_low(3), None, None))
            step(0, 2, between=(None, lambda: w1_low(4), None, None))
            step(0, 3, early=(None, None, None, lambda: q_low(2)), between=(None, lambda: w1_low(5), None, None))
            step(0, 4, between=(None, lambda: w1_low(6), route_gates, None))
            step(0, 5, between=(None, lambda: w1_low(7), route_experts, None))
            step(0, 6, between=(None, lambda: xgT_low(0, 0), None, None))

            def l1_copy(b, u):
                i = b * TB + u
                dve.wait_ge(Z["l1_done"], i + 1)
                if not (exact(b) and i < 2):
                    dve.wait_ge(Z["midT_done"], i - 1)
                dve.tensor_copy(mid[:, u % 2, :], ps_s[:, u % 2, :]).then_inc(Z["l1_copied"], 1)

            def y_add(b, u, e):
                i = b * TB + u
                h = (u - 2) % TB // 2
                dve.wait_ge(Z["y_done"], i - 1)
                if u % 2 == 0 and not (exact(b) and i < 6):
                    dve.wait_ge(s_y[h], b * 16 if h == 0 else (b - 1) * 16)
                dve.tensor_tensor(y_sb[:, (u - 2) % TB, :], ps_s[:, 2 + u % 2, 0:D], b2_sb[:, bass.ds(e, 1), :].rearrange("p a d -> p (a d)"),
                                  ALU.add).then_inc(Z["y_ready"], 1)

            def moe_batch(b, last=False):
                start = 2 if exact(b) and b == 0 else 0
                experts = [None] * start + expert_of(dve, b * TB - 2 + start, TB - start)
                for u in range(TB):
                    if not (last and u == TB - 1):
                        l1_copy(b, u)
                    if u >= start:
                        y_add(b, u, experts[u])
                    if u == 0:
                        xgT_low(b, 1)
                    if u == 2 and not last:
                        xgT_low(b + 1, 0)

            dve.wait_ge(Z["experts_ready"], 1)
            moe_batch(0)
            moe_batch(1)
            with dve.Fori(2, MB - 1) as b:
                moe_batch(b)
            moe_batch(MB - 1, last=True)
            y_add(MB, 0, expert_of(dve, MT - 1, 1)[0])

            def row(t, j):
                return t[:, bass.ds(j, 1), :].rearrange("p a d -> p (a d)")

            def weigh(j, zb, k):
                for t in range(2):
                    dve.wait_ge(s_z[zb + t], k * 32 + 32)
                    dve.tensor_scalar(row(moe, j + t), z[:, zb + t, 0, :], gate1[:, bass.ds(j + t, 1)], None,
                                      ALU.mult).then_inc(Z["moe_link"], 1)

            def combine(j, zb):
                for t in range(2):
                    dve.wait_ge(Z["moe_link"], j + (t + 1))
                    dve.scalar_tensor_tensor(out=row(moe, j + t), in0=z[:, zb + t, 1, :], scalar=gate2[:, bass.ds(j + t, 1)],
                                             in1=row(moe, j + t), op0=ALU.mult, op1=ALU.add).then_inc(Z["combined"], 1)

            with dve.Fori(1, NR - 1) as it:
                for n in range(TB):
                    j = it * ZB + (2 * n - ZB)
                    step(it, 3 + n, early=(None, None, None, (lambda: q_low(it + 2)) if n == 0 else None),
                         between=(None, None, lambda: weigh(j, 2 * n, it - 1), lambda: combine(j, 2 * n)))
            step(NR - 1, 3)
            step(NR - 1, 4, scores=False)
            dve.wait_ge(Z["x_biased"], 2)

            def add_out(r):
                dve.wait_ge(Z["out_done"], r + 1)
                dve.tensor_tensor(x_sb[:, TB * r:TB * (r + 1), :], ps_s[:, r, :].rearrange("p (j e) -> p j e", e=D),
                                  x_sb[:, TB * r:TB * (r + 1), :], ALU.add).then_inc(Z["out_added"], 1)

            link("sums", dve.tensor_reduce(rinv[:, :], sums[:, :].rearrange("p (j b) -> p j b", b=NR), AX.X, ALU.add))
            link("sums", dve.reciprocal(rinv[:, :], rinv[:, :]))
            for r in range(NR):
                dve.wait_ge(Z["oTT_done"], r + 1)
                if r >= 2:
                    dve.wait_ge(Z["out_done"], r - 1)
                dve.tensor_tensor(o_sb[:, r % 2, :, :], ps_t[:, r % 2, :].rearrange("q (j d) -> q j d", d=D),
                                  rinv[:, TB * r:TB * (r + 1)].unsqueeze(2).to_broadcast([P, TB, D]),
                                  ALU.mult).then_inc(Z["o_ready"], 1)
                if r >= 1:
                    add_out(r - 1)
            add_out(NR - 1)

        @block.tensor
        def _(pe):
            def product(dst, lhs, rhs, start=True, stop=True):
                (lh, ll), (rh, rl) = lhs, rhs
                pe.matmul(dst, lh, rh, start=start, stop=False)
                pe.matmul(dst, lh, rl, start=False, stop=False)
                return pe.matmul(dst, ll, rh, start=False, stop=stop)

            def xnT(cols):
                return xnT_hi[:, cols], xnT_lo[:, cols]

            pe.wait_ge(Z["ones_ready"], 1)

            def keep_warm(n):
                for k in range(n):
                    pe.matmul(ps_t[:, 0, 0:P], ones[:, :], ones[:, :], start=True, stop=True)
            keep_warm(14)

            pe.wait_ge(Z["consts"], 9)
            pe.wait_ge(Z["w_loaded"], 16 * 7)
            pe.transpose(ps_m[:, 2 * D:3 * D], w_raw[:, 4, :], ident[:, :])
            pe.matmul(ps_m[:, 0:D], w_raw[:, 0, :], w_raw[:, 1, :], start=True, stop=True)
            pe.transpose(ps_m[:, 3 * D:3 * D + NE * HC], b1_rows, ident[0:NE * HC, 0:NE * HC])
            pe.transpose(ps_m[:, D:2 * D], w_raw[:, 2, :], ident[:, :]).then_inc(Z["wT_done"], 1)
            pe.transpose(ps_o[:, 0:D], w_raw[:, 3, :], ident[:, :])
            pe.wait_ge(Z["winT_ready"], 1)
            pe.matmul(ps_o[:, D:D + NE], winT, wg_sb[:, :], start=True, stop=True)
            pe.matmul(ps_o[:, D + NE:D + 2 * NE], bin_col[:, 0:1].to_broadcast([P, P]), wg_sb[:, :],
                      start=True, stop=True).then_inc(Z["gate_done"], 1)

            def xn_transpose(r):
                pe.wait_ge(Z["xn_ready"], 2 * (r + 1))
                pe.wait_ge(Z["xn_act_ready"], 2 * (r + 1))
                for j in range(TB):
                    last = pe.transpose(ps_s[:, r, P * j:P * (j + 1)], xn[:, r % 2, j, :], ident[:, :])
                last.then_inc(Z["xT_done"], 1)

            def logits(r):
                pe.wait_ge(Z["xT_lo"], r + 1)
                for j in range(TB * r, TB * (r + 1)):
                    xh, xl = xnT(slice(P * j, P * (j + 1)))
                    g = slice(2 * NE * j, 2 * NE * j + P)
                    pe.matmul(ps_o[:, g], xh, gate_w[:, 0, :], start=True, stop=False)
                    last = pe.matmul(ps_o[:, g], xl, gate_w[:, 1, :], start=False, stop=True)
                return last

            def values(n):
                if n >= 2:
                    pe.wait_ge(Z["rows_ready"], n - 1)
                for k in range(2):
                    j = 2 * n + k
                    last = product(vt_bank(n)[:, k, :, :].rearrange("p t d -> p (t d)"), xnT(slice(P * j, P * (j + 1))),
                                   [t[:, :, :].rearrange("p t d -> p (t d)") for t in (vt_hi, vt_lo)])
                last.then_inc(Z["vt_done"], 1)

            def q_project(it):
                x4 = [t[:, :].rearrange("e (j p) -> e j p", p=P)[:, :, bass.ds(it * PG, PG)] for t in (xnT_hi, xnT_lo)]
                product(q_psum, (mm_hi[:, :], mm_lo[:, :]), x4).then_inc(Z["q_done"], 1)

            keep_warm(5)
            xn_transpose(0)
            keep_warm(4)
            xn_transpose(1)
            keep_warm(3)
            pe.wait_ge(Z["w_lo_ready"], 3)
            logits(0)
            xn_transpose(2)
            logits(1)
            values(0)
            xn_transpose(3)
            logits(2)
            values(1)
            logits(3).then_inc(Z["logits_done"], 1)
            q_project(0)
            values(2)

            def xg_transpose(b, g):
                pe.wait_ge(s_xg[g], (b + 1) * 16)
                if not (exact(b) and b == 0 and g == 0):
                    pe.wait_ge(Z["xgT_lo_ready"], b * 2 + g)
                for k in range(2 * g, 2 * g + 2):
                    last = pe.transpose(ps_m[:, P * k:P * (k + 1)], xg[:, k, :], ident[:, :])
                last.then_inc(Z["xgT_done"], 1)

            def step(it, c, scores=True, tr=True, pv=True, q_next=None, then=None):
                i = it * TB + c
                if scores:
                    if c % TB == 0:
                        pe.wait_ge(Z["q_lo_ready"], it + (c // TB + 1))
                    for b in range(NR):
                        if not (exact(it) and i < 1):
                            pe.wait_ge(Z["exp_done"], (i - 1) * NR + (b + 1))
                        product(ps_s[:, b, :], (q_hi[:, P * (c % TB):P * (c % TB + 1)], q_lo[:, P * (c % TB):P * (c % TB + 1)]),
                                xnT(slice(BK * b, BK * (b + 1)))).then_inc(Z["scores_done"], 1)
                if then is not None:
                    then()
                if q_next is not None:
                    q_project(q_next)
                g = it * 2 + ((c - 3) // 2)
                half = (c - 3) % 2
                for b in range(NR):
                    if tr:
                        if not scores:
                            pe.wait_ge(Z["exp_done"], (i - 1) * NR + (b + 1))
                        if not (exact(it) and i == 1 and b < 2):
                            pe.wait_ge(Z["pt_lo_ready"], (i - 1) * NR + (b - 1))
                        for k in range(TB):
                            at = BK * b + P * k
                            last = pe.transpose(ps_t[:, b % 2, P * k:P * (k + 1)], probs[:, at:at + P], ident[:, :])
                        last.then_inc(Z["pT_done"], 1)
                    if pv:
                        if b == 0 and half == 0:
                            pe.wait_ge(Z["pt_lo_ready"], (g + 1) * (2 * NR))
                            if not (exact(it) and it == 0 and c < 5):
                                pe.wait_ge(Z["oT_copied"], g)
                        G = (c - 3) // 2 % 2
                        for k in range(2):
                            ch = half * (NT // 2) + 2 * b + k
                            last = product(ps_o[:, 0:2 * P], (v_hi[:, ch, :], v_lo[:, ch, :]),
                                           (pt_hi[:, G, ch, :], pt_lo[:, G, ch, :]), start=(ch == 0), stop=(ch == NT - 1))
                        if ch == NT - 1:
                            last.then_inc(Z["pv_done"], 1)

            def prefix():
                pe.wait_ge(Z["both_ready"], 1)
                flat = both[:, :, :].rearrange("p j e -> p (j e)")
                pe.matmul(ps_o[:, BK // 4:BK // 4 + NT * NE], tri[:, :], flat, start=True, stop=True)
                pe.matmul(ps_o[:, BK // 2:BK // 2 + NT * NE], ones[:, :], flat, start=True, stop=True).then_inc(Z["prefix_done"], 1)

            step(0, 0, tr=False, pv=False)
            prefix()
            values(3)
            values(4)

            def last_values():
                for n in range(5, NT // 2):
                    values(n)
                pe.wait_ge(Z["rows_ready"], NT // 2)

            step(0, 1, pv=False, then=last_values)
            step(0, 2, pv=False)
            pe.wait_ge(Z["slots_ready"], 1)
            pe.wait_ge(Z["v_lo_ready"], NT // 2)
            step(0, 3, q_next=1)
            step(0, 4)
            step(0, 5)
            step(0, 6, then=lambda: xg_transpose(0, 0))

            def layer1(b, u, experts):
                e = experts[u]
                if u % 2 == 0:
                    pe.wait_ge(Z["xgT_lo_ready"], b * 2 + (u // 2 + 1))
                at = slice(P * u, P * (u + 1))
                w1e = [t[:, bass.ds(e, 1), :].rearrange("p a h -> p (a h)") for t in (w1_hi, w1_lo)]
                product(ps_s[:, u % 2, :], (xgT_hi[:, at], xgT_lo[:, at]), w1e).then_inc(Z["l1_done"], 1)

            def mid_transpose(b, u):
                i = b * TB + u
                pe.wait_ge(Z["l1_copied"], i)
                for k in range(HC):
                    last = pe.transpose(ps_t[:, (u - 1) % 2, P * k:P * (k + 1)], mid[:, (u - 1) % 2, P * k:P * (k + 1)], ident[:, :])
                last.then_inc(Z["midT_done"], 1)

            def layer2(b, u, e):
                i = b * TB + u
                pe.wait_ge(Z["midT_ready"], (i - 1) * HC)
                if not (exact(b) and i < 4):
                    pe.wait_ge(Z["y_ready"], i - 3)
                for k in range(HC):
                    last = pe.matmul(ps_s[:, 2 + u % 2, 0:D], midT[:, u % 2, k, :],
                                     w2v[:, bass.ds(e, 1), k, :].rearrange("p a d -> p (a d)"),
                                     start=(k == 0), stop=(k == HC - 1))
                last.then_inc(Z["y_done"], 1)

            def moe_batch(b, last=False):
                if exact(b) and b == 0:
                    experts = [None] * 2 + expert_of(pe, 0, TB)
                else:
                    experts = expert_of(pe, b * TB - 2, 2 + TB)
                for u in range(TB):
                    if not (last and u == TB - 1):
                        layer1(b, u, experts[2:])
                    if u == 0:
                        xg_transpose(b, 1)
                    if u == 2 and not last:
                        xg_transpose(b + 1, 0)
                    if exact(b) and b == 0 and u == 1:
                        pe.wait_ge(Z["pt_lo_ready"], 6 * NR)
                    if not (exact(b) and b == 0 and u < 1):
                        mid_transpose(b, u)
                    if exact(b) and b == 0 and u == 2:
                        pe.wait_ge(Z["w2_loaded"], 32)
                        pe.wait_ge(Z["exp_done"], 7 * NR)
                    if not (exact(b) and b == 0 and u < 2):
                        layer2(b, u, experts[u])

            pe.wait_ge(Z["exp_done"], 6 * NR + 2)
            pe.wait_ge(Z["w1_split"], 2)
            pe.wait_ge(Z["w1_late"], NE - EP)
            pe.wait_ge(Z["experts_ready"], 1)
            moe_batch(0)
            with pe.Fori(0, MB // 2 - 1) as h:
                for k in range(2):
                    moe_batch(h * 2 + (k + 1))
            moe_batch(MB - 1, last=True)
            layer2(MB, 0, expert_of(pe, MT - 1, 1)[0])
            pe.wait_ge(Z["l1_copied"], MT)
            pe.wait_ge(Z["y_ready"], MT)
            pe.wait_ge(Z["midT_ready"], MT * HC)

            with pe.Fori(1, NR - 1) as it:
                for n in range(TB):
                    step(it, 3 + n, q_next=it + 1 if n == 0 else None)
            step(NR - 1, 3)
            step(NR - 1, 4, scores=False)
            pe.wait_ge(Z["combined"], NT)
            pe.wait_ge(Z["exp_done"], NT * NR)
            for r in range(NR):
                for k in range(TB):
                    last = pe.transpose(ps_s[:, r, P * k:P * (k + 1)], moe[:, TB * r + k, :], ident[:, :])
                last.then_inc(Z["moeT_done"], 1)

            def o_transpose(r):
                pe.wait_ge(Z["oT_copied"], 2 * r + 2)
                if r >= 2:
                    pe.wait_ge(Z["o_ready"], r - 1)
                for k in range(TB):
                    last = pe.transpose(ps_t[:, r % 2, P * k:P * (k + 1)], oT_all[:, TB * r + k, :], ident[:, :])
                last.then_inc(Z["oTT_done"], 1)

            def project(r):
                pe.wait_ge(Z["moeT_ready"], r + 1)
                for k in range(TB):
                    dst = ps_s[:, r, P * k:P * (k + 1)]
                    pe.matmul(dst, moeT[:, P * (TB * r + k):P * (TB * r + k + 1)], wo_sb[:, :], start=True, stop=False)
                    if k == 0:
                        pe.wait_ge(Z["o_ready"], r + 1)
                    last = pe.matmul(dst, o_sb[:, r % 2, k, :], wpT[:, :], start=False, stop=True)
                last.then_inc(Z["out_done"], 1)

            pe.wait_ge(Z["pt_lo_ready"], NT * NR)
            o_transpose(0)
            o_transpose(1)
            step(NR - 1, 5, scores=False, tr=False)
            project(0)
            project(1)
            o_transpose(2)
            step(NR - 1, 6, scores=False, tr=False)
            project(2)
            o_transpose(3)
            project(3)


_INS = ['L0_attn_x', 'L0_attn_w_qkv', 'L0_attn_w_proj', 'L0_attn_b_proj', 'L0_ffn_W_in', 'L0_ffn_b_in',
        'L0_ffn_W_gate', 'L0_ffn_b_gate', 'L0_ffn_W1', 'L0_ffn_b1', 'L0_ffn_W2', 'L0_ffn_b2', 'L0_ffn_W_out',
        'L0_ffn_b_out']
_OUTS = [((1, 2048, 128), 'float32')]


def kernel(**inputs):
    import numpy as _np
    import concourse.bacc as _bacc
    from concourse import mybir as _mybir
    from concourse.bass_utils import run_bass_kernel_spmd as _run

    nc = _bacc.Bacc("TRN2", target_bir_lowering=False, num_devices=1)
    arrays, args = {}, []
    for name in _INS:
        a = _np.ascontiguousarray(inputs[name])
        arrays[f"in_{name}_dram"] = a
        args.append(nc.dram_tensor(f"in_{name}_dram", a.shape, _mybir.dt.from_np(a.dtype), kind="ExternalInput").ap())
    for i, (shape, dtype) in enumerate(_OUTS):
        dt = _mybir.dt.from_np(_np.dtype(dtype))
        args.append(nc.dram_tensor(f"out_{i}_dram", shape, dt, kind="ExternalOutput").ap())
    attention_moe_kernel(nc, *args)
    r = _run(nc, [arrays], core_ids=[0])
    return r.results[0]["out_0_dram"]
```
